# Optimizing a Trainium2 kernel written in Bass

```python
import numpy as np
import jax
import jax.numpy as jnp

def _softmax(x, axis=-1):
    return jax.nn.softmax(x, axis=axis)

def _gelu(x):
    return jax.nn.gelu(x, approximate=True)

def _silu(x):
    return jax.nn.silu(x)

def _sigmoid(x):
    return jax.nn.sigmoid(x)

def _layernorm(x, axis=-1, eps=1e-05):
    m = jnp.mean(x, axis=axis, keepdims=True)
    v = jnp.var(x, axis=axis, keepdims=True)
    return (x - m) / jnp.sqrt(v + eps)

def _scatter_add(tgt, idx, src, axis=0):
    return tgt.at[idx].add(src)

def _segment_sum(src, seg, n):
    return jax.ops.segment_sum(src, seg, n)
kernel_name = 'mk_seq_preln_d2_jaxref_r8_ea971b'

def setup_inputs(seed: int=0):
    np.random.seed(seed)
    _w = jnp.asarray

    def _L0_attn_setup():
        import jax, jax.numpy as jnp
        import numpy as np
        HIDDEN = 256
        NUM_HEADS = 6
        HEAD_V = 64
        VALUE_DIM = NUM_HEADS * HEAD_V
        CONV_K = 4
        PHASE_BASE = 10000.0
        EPS = 1e-05

        def _causal_depthwise_conv(x, w):
            B, T, C = x.shape
            K = w.shape[1]
            xp = jnp.pad(x, ((0, 0), (K - 1, 0), (0, 0)))
            y = jnp.zeros_like(x)
            for j in range(K):
                y = y + xp[:, j:j + T, :] * w[:, j]
            return y

        def _rotate(x, ang):
            cos = jnp.cos(ang)
            sin = jnp.sin(ang)
            xe = x[..., ::2]
            xo = x[..., 1::2]
            ye = xe * cos - xo * sin
            yo = xo * cos + xe * sin
            return jnp.stack([ye, yo], axis=-1).reshape(x.shape)

        def _forward(hidden_states, Wq, Wk, Wv, Wa, Wb, Wg, Wo, conv_q, conv_k, conv_v, rms_w):
            B, T, _ = hidden_states.shape
            H, D = (NUM_HEADS, HEAD_V)
            inv_freq = 1.0 / PHASE_BASE ** (jnp.arange(0, D, 2, dtype=jnp.float32) / D)
            q = _causal_depthwise_conv(hidden_states @ Wq, conv_q).reshape(B, T, H, D)
            k = _causal_depthwise_conv(hidden_states @ Wk, conv_k).reshape(B, T, H, D)
            v = _causal_depthwise_conv(hidden_states @ Wv, conv_v).reshape(B, T, H, D)
            theta = q[..., ::2] * inv_freq
            psi = k[..., ::2] * inv_freq
            phi = theta - jnp.concatenate([jnp.zeros_like(theta[:, :1]), theta[:, :-1]], axis=1)
            alpha = jax.nn.sigmoid(hidden_states @ Wa)
            beta = jax.nn.sigmoid(hidden_states @ Wb)
            tm = lambda a: jnp.moveaxis(a, 1, 0)
            xs = (tm(theta), tm(psi), tm(phi), tm(v), tm(alpha), tm(beta))

            def step(state, inp):
                th, ps, ph, vt, at, bt = inp
                retained = _rotate(state, ph) * at[..., None]
                write = _rotate(vt, ps)
                new_state = retained + bt[..., None] * write
                out_t = _rotate(new_state, -th)
                return (new_state, out_t)
            state0 = jnp.zeros((B, H, D), hidden_states.dtype)
            _, out = jax.lax.scan(step, state0, xs)
            out = jnp.moveaxis(out, 0, 1)
            g = (hidden_states @ Wg).reshape(B, T, H, D)
            rms = jax.lax.rsqrt(jnp.mean(jnp.square(out), axis=-1, keepdims=True) + EPS)
            o = out * rms * rms_w * jax.nn.silu(g)
            return o.reshape(B, T, VALUE_DIM) @ Wo
        key = jax.random.key(seed)
        ks = jax.random.split(key, 12)
        s = 0.02
        return {'hidden_states': jax.random.normal(ks[0], (2, 256, HIDDEN), jnp.float32), 'Wq': jax.random.normal(ks[1], (HIDDEN, VALUE_DIM), jnp.float32) * s, 'Wk': jax.random.normal(ks[2], (HIDDEN, VALUE_DIM), jnp.float32) * s, 'Wv': jax.random.normal(ks[3], (HIDDEN, VALUE_DIM), jnp.float32) * s, 'Wa': jax.random.normal(ks[4], (HIDDEN, NUM_HEADS), jnp.float32) * s, 'Wb': jax.random.normal(ks[5], (HIDDEN, NUM_HEADS), jnp.float32) * s, 'Wg': jax.random.normal(ks[6], (HIDDEN, VALUE_DIM), jnp.float32) * s, 'Wo': jax.random.normal(ks[7], (VALUE_DIM, HIDDEN), jnp.float32) * s, 'conv_q': jax.random.normal(ks[8], (VALUE_DIM, CONV_K), jnp.float32) * s, 'conv_k': jax.random.normal(ks[9], (VALUE_DIM, CONV_K), jnp.float32) * s, 'conv_v': jax.random.normal(ks[10], (VALUE_DIM, CONV_K), jnp.float32) * s, 'rms_w': jnp.ones((HEAD_V,), jnp.float32)}
    _L0_attn_in = _L0_attn_setup()

    def _L0_ffn_setup():
        import jax, jax.numpy as jnp
        import numpy as np
        B, S, H = (4, 128, 256)
        E = 16
        K = 2
        I = 128
        N_SHARED = 2
        I_SHARED = I * N_SHARED
        RATIO = 0.1
        EPS = 1e-09

        def _swiglu(x, wg, wu, wd):
            return jax.nn.silu(x @ wg) * (x @ wu) @ wd
        key = jax.random.key(seed)
        ks = jax.random.split(key, 9)
        scale = 0.02
        x = jax.random.normal(ks[0], (B, S, H), dtype=jnp.float32)
        centroids = jax.random.normal(ks[1], (E, H), dtype=jnp.float32)
        gate_bias = jnp.zeros((E,), dtype=jnp.float32)
        wg_s = jax.random.normal(ks[2], (H, I_SHARED), dtype=jnp.float32) * scale
        wu_s = jax.random.normal(ks[3], (H, I_SHARED), dtype=jnp.float32) * scale
        wd_s = jax.random.normal(ks[4], (I_SHARED, H), dtype=jnp.float32) * scale
        wg = jax.random.normal(ks[5], (E, H, I), dtype=jnp.float32) * scale
        wu = jax.random.normal(ks[6], (E, H, I), dtype=jnp.float32) * scale
        wd = jax.random.normal(ks[7], (E, I, H), dtype=jnp.float32) * scale
        return {'x': x, 'centroids': centroids, 'gate_bias': gate_bias, 'wg_s': wg_s, 'wu_s': wu_s, 'wd_s': wd_s, 'wg': wg, 'wu': wu, 'wd': wd}
    _L0_ffn_in = _L0_ffn_setup()

    def _L1_attn_setup():
        import jax, jax.numpy as jnp
        import numpy as np
        key = jax.random.key(seed)
        ks = jax.random.split(key, 5)
        B, S, D = (1, 512, 256)
        H, Dh = (16, 128)
        scale = 1.0 / np.sqrt(D).astype(np.float32)
        return {'x': jax.random.normal(ks[0], (B, S, D), dtype=jnp.float32), 'W_K': jax.random.normal(ks[1], (H, Dh, D), dtype=jnp.float32) * scale, 'W_Q': jax.random.normal(ks[2], (H, Dh, D), dtype=jnp.float32) * scale, 'W_V': jax.random.normal(ks[3], (H, Dh, D), dtype=jnp.float32) * scale, 'W_O': jax.random.normal(ks[4], (D, H * Dh), dtype=jnp.float32) * scale}
    _L1_attn_in = _L1_attn_setup()

    def _L1_ffn_setup():
        import jax, jax.numpy as jnp
        import numpy as np
        HIDDEN = 256
        INTER = 688
        LUT_SIZE = 16

        def _ghost_linear(x, idx, lut):
            w = lut[idx]
            return jnp.einsum('bsh,oh->bso', x, w)
        key = jax.random.key(seed)
        k_x, k_lut, k_g, k_u, k_d = jax.random.split(key, 5)
        x = jax.random.normal(k_x, (2, 512, HIDDEN), dtype=jnp.float32)
        lut = jax.random.normal(k_lut, (LUT_SIZE,), dtype=jnp.float32) * 0.02
        gate_idx = jax.random.randint(k_g, (INTER, HIDDEN), 0, LUT_SIZE, dtype=jnp.int32)
        up_idx = jax.random.randint(k_u, (INTER, HIDDEN), 0, LUT_SIZE, dtype=jnp.int32)
        down_idx = jax.random.randint(k_d, (HIDDEN, INTER), 0, LUT_SIZE, dtype=jnp.int32)
        return {'x': x, 'lut': lut, 'gate_idx': gate_idx, 'up_idx': up_idx, 'down_idx': down_idx}
    _L1_ffn_in = _L1_ffn_setup()
    _d = {'L0_attn_hidden_states': _L0_attn_in['hidden_states'], 'L0_attn_Wq': _L0_attn_in['Wq'], 'L0_attn_Wk': _L0_attn_in['Wk'], 'L0_attn_Wv': _L0_attn_in['Wv'], 'L0_attn_Wa': _L0_attn_in['Wa'], 'L0_attn_Wb': _L0_attn_in['Wb'], 'L0_attn_Wg': _L0_attn_in['Wg'], 'L0_attn_Wo': _L0_attn_in['Wo'], 'L0_attn_conv_q': _L0_attn_in['conv_q'], 'L0_attn_conv_k': _L0_attn_in['conv_k'], 'L0_attn_conv_v': _L0_attn_in['conv_v'], 'L0_attn_rms_w': _L0_attn_in['rms_w'], 'L0_ffn_centroids': _L0_ffn_in['centroids'], 'L0_ffn_gate_bias': _L0_ffn_in['gate_bias'], 'L0_ffn_wg_s': _L0_ffn_in['wg_s'], 'L0_ffn_wu_s': _L0_ffn_in['wu_s'], 'L0_ffn_wd_s': _L0_ffn_in['wd_s'], 'L0_ffn_wg': _L0_ffn_in['wg'], 'L0_ffn_wu': _L0_ffn_in['wu'], 'L0_ffn_wd': _L0_ffn_in['wd'], 'L1_attn_W_K': _L1_attn_in['W_K'], 'L1_attn_W_Q': _L1_attn_in['W_Q'], 'L1_attn_W_V': _L1_attn_in['W_V'], 'L1_attn_W_O': _L1_attn_in['W_O'], 'L1_ffn_lut': _L1_ffn_in['lut'], 'L1_ffn_gate_idx': _L1_ffn_in['gate_idx'], 'L1_ffn_up_idx': _L1_ffn_in['up_idx'], 'L1_ffn_down_idx': _L1_ffn_in['down_idx']}
    _x0 = _d['L0_attn_hidden_states']
    _d['L0_attn_hidden_states'] = jax.random.normal(jax.random.fold_in(jax.random.key(seed), 1), (8, 512, 256), dtype=_x0.dtype)
    del _x0
    return _d

def reference(L0_attn_hidden_states, L0_attn_Wq, L0_attn_Wk, L0_attn_Wv, L0_attn_Wa, L0_attn_Wb, L0_attn_Wg, L0_attn_Wo, L0_attn_conv_q, L0_attn_conv_k, L0_attn_conv_v, L0_attn_rms_w, L0_ffn_centroids, L0_ffn_gate_bias, L0_ffn_wg_s, L0_ffn_wu_s, L0_ffn_wd_s, L0_ffn_wg, L0_ffn_wu, L0_ffn_wd, L1_attn_W_K, L1_attn_W_Q, L1_attn_W_V, L1_attn_W_O, L1_ffn_lut, L1_ffn_gate_idx, L1_ffn_up_idx, L1_ffn_down_idx):

    def _L0_attn_ref(hidden_states, Wq, Wk, Wv, Wa, Wb, Wg, Wo, conv_q, conv_k, conv_v, rms_w):
        import jax, jax.numpy as jnp
        import numpy as np
        HIDDEN = 256
        NUM_HEADS = 6
        HEAD_V = 64
        VALUE_DIM = NUM_HEADS * HEAD_V
        CONV_K = 4
        PHASE_BASE = 10000.0
        EPS = 1e-05

        def _causal_depthwise_conv(x, w):
            B, T, C = x.shape
            K = w.shape[1]
            xp = jnp.pad(x, ((0, 0), (K - 1, 0), (0, 0)))
            y = jnp.zeros_like(x)
            for j in range(K):
                y = y + xp[:, j:j + T, :] * w[:, j]
            return y

        def _rotate(x, ang):
            cos = jnp.cos(ang)
            sin = jnp.sin(ang)
            xe = x[..., ::2]
            xo = x[..., 1::2]
            ye = xe * cos - xo * sin
            yo = xo * cos + xe * sin
            return jnp.stack([ye, yo], axis=-1).reshape(x.shape)

        def _forward(hidden_states, Wq, Wk, Wv, Wa, Wb, Wg, Wo, conv_q, conv_k, conv_v, rms_w):
            B, T, _ = hidden_states.shape
            H, D = (NUM_HEADS, HEAD_V)
            inv_freq = 1.0 / PHASE_BASE ** (jnp.arange(0, D, 2, dtype=jnp.float32) / D)
            q = _causal_depthwise_conv(hidden_states @ Wq, conv_q).reshape(B, T, H, D)
            k = _causal_depthwise_conv(hidden_states @ Wk, conv_k).reshape(B, T, H, D)
            v = _causal_depthwise_conv(hidden_states @ Wv, conv_v).reshape(B, T, H, D)
            theta = q[..., ::2] * inv_freq
            psi = k[..., ::2] * inv_freq
            phi = theta - jnp.concatenate([jnp.zeros_like(theta[:, :1]), theta[:, :-1]], axis=1)
            alpha = jax.nn.sigmoid(hidden_states @ Wa)
            beta = jax.nn.sigmoid(hidden_states @ Wb)
            tm = lambda a: jnp.moveaxis(a, 1, 0)
            xs = (tm(theta), tm(psi), tm(phi), tm(v), tm(alpha), tm(beta))

            def step(state, inp):
                th, ps, ph, vt, at, bt = inp
                retained = _rotate(state, ph) * at[..., None]
                write = _rotate(vt, ps)
                new_state = retained + bt[..., None] * write
                out_t = _rotate(new_state, -th)
                return (new_state, out_t)
            state0 = jnp.zeros((B, H, D), hidden_states.dtype)
            _, out = jax.lax.scan(step, state0, xs)
            out = jnp.moveaxis(out, 0, 1)
            g = (hidden_states @ Wg).reshape(B, T, H, D)
            rms = jax.lax.rsqrt(jnp.mean(jnp.square(out), axis=-1, keepdims=True) + EPS)
            o = out * rms * rms_w * jax.nn.silu(g)
            return o.reshape(B, T, VALUE_DIM) @ Wo
        return _forward(hidden_states, Wq, Wk, Wv, Wa, Wb, Wg, Wo, conv_q, conv_k, conv_v, rms_w)

    def _L0_ffn_ref(x, centroids, gate_bias, wg_s, wu_s, wd_s, wg, wu, wd):
        import jax, jax.numpy as jnp
        import numpy as np
        B, S, H = (4, 128, 256)
        E = 16
        K = 2
        I = 128
        N_SHARED = 2
        I_SHARED = I * N_SHARED
        RATIO = 0.1
        EPS = 1e-09

        def _swiglu(x, wg, wu, wd):
            return jax.nn.silu(x @ wg) * (x @ wu) @ wd
        shared = _swiglu(x, wg_s, wu_s, wd_s) * RATIO
        affinity = jax.nn.sigmoid(jnp.einsum('bsh,eh->bse', x, centroids))
        biased = affinity + gate_bias
        _, top_idx = jax.lax.top_k(biased, K)
        top_aff = jnp.take_along_axis(affinity, top_idx, axis=-1)
        weights = top_aff / (top_aff.sum(-1, keepdims=True) + EPS)
        mask = (jax.nn.one_hot(top_idx, E, dtype=x.dtype) * weights[..., None]).sum(-2)
        routed = jnp.zeros_like(x)
        for e in range(E):
            routed = routed + mask[..., e:e + 1] * _swiglu(x, wg[e], wu[e], wd[e])
        return shared + routed

    def _L1_attn_ref(x, W_K, W_Q, W_V, W_O):
        import jax, jax.numpy as jnp
        import numpy as np
        b, pos, d_model = x.shape
        d_head = W_K.shape[1]
        k = jnp.einsum('ihd,bpd->biph', W_K, x)
        q = jnp.einsum('ihd,bpd->biph', W_Q, x)
        v = jnp.einsum('ihd,bpd->biph', W_V, x)
        scores = jnp.einsum('biph,biqh->biqp', k, q)
        mask = jnp.tril(jnp.ones((pos, pos), dtype=x.dtype))
        masked = scores * mask - jnp.float32(10000000000.0) * (1.0 - mask)
        attn = jax.nn.softmax(masked / jnp.sqrt(jnp.float32(d_head)), axis=-1)
        z = jnp.einsum('biqp,biph->biqh', attn, v)
        z_flat = jnp.transpose(z, (0, 2, 1, 3)).reshape(b, pos, -1)
        out = jnp.einsum('df,bqf->bqd', W_O, z_flat)
        return out

    def _L1_ffn_ref(x, lut, gate_idx, up_idx, down_idx):
        import jax, jax.numpy as jnp
        import numpy as np
        HIDDEN = 256
        INTER = 688
        LUT_SIZE = 16

        def _ghost_linear(x, idx, lut):
            w = lut[idx]
            return jnp.einsum('bsh,oh->bso', x, w)
        gate = _ghost_linear(x, gate_idx, lut)
        up = _ghost_linear(x, up_idx, lut)
        h = jax.nn.silu(gate) * up
        return _ghost_linear(h, down_idx, lut)
    x = L0_attn_hidden_states
    x = x + _L0_attn_ref(_layernorm(x, axis=-1), L0_attn_Wq, L0_attn_Wk, L0_attn_Wv, L0_attn_Wa, L0_attn_Wb, L0_attn_Wg, L0_attn_Wo, L0_attn_conv_q, L0_attn_conv_k, L0_attn_conv_v, L0_attn_rms_w)
    x = x + _L0_ffn_ref(_layernorm(x, axis=-1), L0_ffn_centroids, L0_ffn_gate_bias, L0_ffn_wg_s, L0_ffn_wu_s, L0_ffn_wd_s, L0_ffn_wg, L0_ffn_wu, L0_ffn_wd)
    x = x + _L1_attn_ref(_layernorm(x, axis=-1), L1_attn_W_K, L1_attn_W_Q, L1_attn_W_V, L1_attn_W_O)
    x = x + _L1_ffn_ref(_layernorm(x, axis=-1), L1_ffn_lut, L1_ffn_gate_idx, L1_ffn_up_idx, L1_ffn_down_idx)
    return x

_drawn_inputs = setup_inputs


def setup_inputs(seed=0):
    import zlib

    import numpy as np

    out = dict(_drawn_inputs(seed))
    spreads = {'L0_attn_rms_w': (1.0, 0.6), 'L0_ffn_gate_bias': (0.0, 0.732)}
    factors = {'L0_attn_Wq': 8.0,
     'L0_attn_Wk': 8.0,
     'L0_attn_Wa': 8.0,
     'L0_attn_Wb': 7.702,
     'L0_attn_conv_q': 8.0,
     'L0_attn_conv_k': 8.0,
     'L0_ffn_centroids': 7.125,
     'L0_ffn_wg_s': 8.0,
     'L0_ffn_wu_s': 8.0,
     'L0_ffn_wd_s': 8.0,
     'L0_ffn_wg': 5.984,
     'L0_ffn_wu': 5.907,
     'L0_ffn_wd': 5.932,
     'L1_ffn_lut': 3.786}
    for name, (base, spread) in spreads.items():
        noise = np.random.default_rng([zlib.crc32(name.encode()), seed]).standard_normal(out[name].shape)
        drawn = base * np.exp(spread * noise) if base else spread * noise
        out[name] = jnp.asarray(drawn.astype(out[name].dtype))
    for name, factor in factors.items():
        out[name] = (out[name] * factor).astype(out[name].dtype)
    return out
```

```python
from contextlib import ExitStack
import math

import numpy as np
import concourse.bass as bass
from concourse import mybir

ALU = mybir.AluOpType
ACT = mybir.ActivationFunctionType
F32 = mybir.dt.float32
BF16 = mybir.dt.bfloat16
I32 = mybir.dt.int32
AX_X = mybir.AxisListType.X

P = 128
NB, T, D = 8, 512, 256
NT = T // P
KD = D // P
HEADS0, PAIRS = 6, 32
HALF = HEADS0 * PAIRS // 2
TAPS = 4
EPS = 1e-5
NEXP, NSHARED = 16, 2
NE = NEXP + NSHARED
SHARED_RATIO = 0.1
NH, DH = 16, 128
SCALE = 1.0 / math.sqrt(DH)
NEG = -1e10
INTER = 688
MT = [(m * P, min(P, INTER - m * P)) for m in range((INTER + P - 1) // P)]
NM = len(MT)
LUTN = 16
FW = KD * INTER * 2 + NM * D
LC = FW // NB

TWO_PI = 2 * math.pi
ROUND = 1.5 * 2.0 ** 23
PI_HI = 6.28125
PI_LO = TWO_PI - PI_HI
PI_MAX = 3.1415925
RSQRT_SEED = float(0x5F3759DF)
START = 1
LN_LINKS = 14
L0_LINKS = 50
RC_LINKS = 19


def two_layer_program(nc, x_in, w0, wab, cw, invf, rmsw, wo0, cent, gbias, wexp, iota16, lutk, wqkv, wo1, fidx, lut, out):
    ctx = ExitStack()
    with ctx:
        def sb(name, shape, dt=F32):
            return ctx.enter_context(nc.sbuf_tensor(name, shape, dt))

        def sem(name):
            return ctx.enter_context(nc.semaphore(name))

        x1 = nc.dram_tensor("x1_between_stages", [NB, T, D], F32, kind="Internal").ap()
        bank = [ctx.enter_context(nc.psum_tensor(f"bank{i}", [P, 512], F32)) for i in range(8)]

        ident = sb("ident", [P, P])
        ident_bf = sb("ident_bf", [P, P], BF16)
        causal = sb("causal", [P, P], BF16)
        half_pi = sb("half_pi", [P, 1])
        headsum = sb("headsum", [HALF, 3])
        w0s = sb("w0s", [P, KD, 6, 2, HALF])
        wabs = sb("wabs", [P, KD, 2, HEADS0])
        wabr = sb("wabr", [P, KD, 2, 2, HALF])
        cws = sb("cws", [HALF, 4, 2, TAPS])
        invfs = sb("invfs", [HALF, 1])
        rmsws = sb("rmsws", [HALF, 2])
        wo0s = sb("wo0s", [HALF, 2, 2, D])
        cents = sb("cents", [P, KD, NEXP])
        gbiass = sb("gbiass", [P, NT, NEXP])
        iotas = sb("iotas", [P, NT, NEXP])
        lutks = sb("lutks", [P, NE])
        luts = sb("luts", [P, NE])
        fidxs = sb("fidxs", [P, FW], I32)
        fws = sb("fws", [P, FW])
        ftmp = sb("ftmp", [P, LC])
        f_gate = fws[:, 0:KD * INTER].rearrange("p (k n) -> p k n", k=KD)
        f_up = fws[:, KD * INTER:2 * KD * INTER].rearrange("p (k n) -> p k n", k=KD)
        f_down = fws[:, 2 * KD * INTER:].rearrange("p (m n) -> p m n", m=NM)

        xin = sb("xin", [P, NT, D])
        xr = sb("xr", [P, NT, D])
        xn = sb("xn", [P, NT, D])
        hT = sb("hT", [P, KD, T])
        stats = sb("stats", [P, NT, 6])
        mv = sb("mv", [P, NT, 2])
        va = sb("va", [P, NT * HEADS0])
        ry = sb("ry", [P, NT * HEADS0])
        rt = sb("rt", [P, NT * HEADS0])
        ang = sb("ang", [HALF, 2, T])
        turns = sb("turns", [HALF, 2, T])
        ve = sb("ve", [HALF, 2, T])
        vo = sb("vo", [HALF, 2, T])
        al = sb("al", [HALF, 2, T])
        be = sb("be", [HALF, 2, T])
        ge = sb("ge", [HALF, 2, T])
        go = sb("go", [HALF, 2, T])
        sn = sb("sn", [HALF, 2, T])
        cs = sb("cs", [HALF, 2, T])
        ab = turns
        t1 = sb("t1", [HALF, 2, T])
        t2 = sb("t2", [HALF, 2, T])
        t3 = sb("t3", [HALF, 2, T])
        t4 = sb("t4", [HALF, 2, T])
        oe = sb("oe", [HALF, 2, T])
        oo = sb("oo", [HALF, 2, T])
        rexp = sb("rexp", [P, NT, HEADS0, PAIRS])
        we = [sb(f"we{i}", [P, 3 * D]) for i in range(2)]
        aff = sb("aff", [P, NT, NEXP])
        bia = sb("bia", [P, NT, NEXP])
        r1 = sb("r1", [P, NT, NEXP])
        r2 = sb("r2", [P, NT, NEXP])
        m1 = sb("m1", [P, NT])
        pick = sb("pick", [P, NT, NEXP])
        mask = sb("mask", [P, NT, NE])
        sg = [sb(f"sg{i}", [P, T]) for i in range(2)]
        act = [sb(f"act{i}", [P, T]) for i in range(2)]
        wh = [sb(f"wh{i}", [P, 3, KD, DH]) for i in range(2)]
        who = [sb(f"who{i}", [P, D]) for i in range(2)]
        qs = sb("qs", [P, T])
        ks = sb("ks", [P, T])
        vs = [sb(f"vs{i}", [P, NT, DH]) for i in range(2)]
        pr = sb("pr", [P, NT, T])
        pt = sb("pt", [P, 3, T])
        zs = sb("zs", [P, T])
        mx = sb("mx", [P, NT])
        nbias = sb("nbias", [P, NT])
        rsum = sb("rsum", [P, NT])
        rinv = sb("rinv", [P, NT])
        fa = sb("fa", [P, NM, T])
        fsg = [sb(f"fsg{i}", [P, T]) for i in range(2)]

        s_const = sem("consts_loaded")
        s_made = sem("consts_made")
        s_made2 = sem("consts_selected")
        s_setup = sem("setup_by_vector")
        s_set = sem("setup_chain")
        s_x0 = sem("x_loaded_stage1")
        s_x0free = sem("x_taken_stage1")
        s_x1 = sem("x_loaded_stage2")
        s_x1free = sem("x_taken_stage2")
        s_st1 = sem("x1_stored")
        s_st2 = sem("out_stored")
        s_kept1 = sem("residual_stored_stage1")
        s_kept2 = sem("residual_stored_stage2")
        s_xn = [sem(f"ln{n}_normalised") for n in range(4)]
        s_hTp = [sem(f"ln{n}_transposed") for n in range(4)]
        s_hTa = [sem(f"ln{n}_copied_by_scalar") for n in range(4)]
        s_hTv = [sem(f"ln{n}_copied_by_vector") for n in range(4)]
        s_lnc = [sem(f"ln{n}_chain") for n in range(4)]
        s_xdone = [sem(f"sublayer{n}_added") for n in range(4)]
        s_pv = sem("l0_projected_for_vector")
        s_pa = sem("l0_projected_for_scalar")
        s_cv = sem("l0_conv_done")
        s_ga = sem("l0_gates_read")
        s_gate = sem("l0_alpha_beta_tanh")
        s_ab = sem("l0_alpha_beta")
        s_rng = sem("l0_angle_reduced")
        s_abs = sem("l0_angle_abs")
        s_trig = sem("l0_sin_cos")
        s_scan = sem("l0_scanned")
        s_sq = sem("l0_squares")
        s_ms = sem("l0_square_sums")
        s_re = sem("l0_rms_spread")
        s_rT = sem("l0_rms_transposed")
        s_y = sem("l0_gated")
        s_o0 = sem("l0_out_product")
        s_l0 = sem("l0_chain")
        s_lg = sem("router_logits")
        s_lgc = sem("router_logits_clamped")
        s_ex = sem("router_exp")
        s_mask = sem("router_mask")
        s_rc = sem("router_chain")
        s_w = [sem(f"expert_weights{i}") for i in range(2)]
        s_gu = sem("expert_gate_product")
        s_up = sem("expert_up_product")
        s_silu = sem("expert_silu")
        s_act = sem("expert_activation")
        s_dn = sem("expert_down_product")
        s_acc = sem("expert_added")
        s_lut = sem("lut_chain")
        s_wh = [sem(f"head_qkv_weights{i}") for i in range(2)]
        s_wo = [sem(f"head_out_weights{i}") for i in range(2)]
        s_q = sem("q_product")
        s_k = sem("k_product")
        s_v = sem("v_product")
        s_qe = sem("q_copied")
        s_ke = sem("k_copied")
        s_ve = sem("v_copied")
        s_s = sem("scores")
        s_mx = sem("score_max")
        s_nb = sem("exp_bias")
        s_e = sem("exps")
        s_t = sem("probs_transposed")
        s_ta = sem("probs_copied_by_scalar")
        s_tv = sem("probs_copied_by_vector")
        s_z = sem("z_product")
        s_ze = sem("z_copied")
        s_o = sem("out_product")
        s_ob = sem("out_product_added")
        s_ri = sem("row_sum_inverted")
        s_fg = sem("ffn_gate_product")
        s_fu = sem("ffn_up_product")
        s_fs = sem("ffn_silu")
        s_fa = sem("ffn_activation")
        s_fd = sem("ffn_down_product")

        CONST_DMAS = 12
        block = ctx.enter_context(nc.Block())

        def rows(ap):
            return ap.rearrange("(n p) d -> p n d", p=P)

        def score(i):
            if i == 0:
                return bank[2][:, 384:512]
            if i == 2:
                return bank[2][:, 0:384]
            return bank[3 if i == 1 else 4][:, 0:(i + 1) * P]

        @block.sync
        def _(sp):
            for dst, src in ((w0s, w0), (wabs, wab), (cws, cw), (invfs, invf), (rmsws, rmsw), (wo0s, wo0),
                             (cents, cent), (gbiass, gbias), (iotas, iota16), (lutks, lutk), (luts, lut),
                             (fidxs, fidx)):
                sp.dma_start(dst[:], src).then_inc(s_const, 16)

            with sp.Fori(0, NB) as b:
                sp.wait_ge(s_x0free, b + START)
                sp.dma_start(xin[:], rows(x_in[bass.ds(b, 1), :, :].rearrange("a t d -> (a t) d"))).then_inc(s_x0, 16)
                sp.wait_ge(s_dn, b * NE + START)
                for p in range(2):
                    sp.dma_start(we[p][:], wexp[p]).then_inc(s_w[p], 16)
                with sp.Fori(1, NE // 2) as i:
                    for p in range(2):
                        sp.wait_ge(s_dn, b * NE + 2 * i + p - 1 + START)
                        sp.dma_start(we[p][:], wexp[bass.ds(2 * i + p, 1), :, :].rearrange("a p n -> (a p) n")
                                     ).then_inc(s_w[p], 16)
            sp.wait_ge(s_st1, 16 * NB)
            with sp.Fori(0, NB) as b:
                sp.wait_ge(s_x1free, b + START)
                sp.dma_start(xin[:], rows(x1[bass.ds(b, 1), :, :].rearrange("a t d -> (a t) d"))).then_inc(s_x1, 16)
                sp.wait_ge(s_o, b * NH + START)
                for p in range(2):
                    sp.dma_start(wh[p][:].rearrange("p c k n -> p (c k n)"), wqkv[p]).then_inc(s_wh[p], 16)
                    sp.dma_start(who[p][:], wo1[p]).then_inc(s_wo[p], 16)
                with sp.Fori(1, NH // 2) as i:
                    for p in range(2):
                        sp.wait_ge(s_v, b * NH + 2 * i + p - 1)
                        sp.dma_start(wh[p][:].rearrange("p c k n -> p (c k n)"),
                                     wqkv[bass.ds(2 * i + p, 1), :, :].rearrange("a p n -> (a p) n")
                                     ).then_inc(s_wh[p], 16)
                        sp.wait_ge(s_o, b * NH + 2 * i + p - 1 + START)
                        sp.dma_start(who[p][:], wo1[bass.ds(2 * i + p, 1), :, :].rearrange("a p n -> (a p) n")
                                     ).then_inc(s_wo[p], 16)

        @block.gpsimd
        def _(pool):
            for s in (s_kept1, s_kept2):
                pool.sem_inc(s, START)
            pool.memset(ident[:], 0.0).then_inc(s_made, 1)
            pool.memset(ident_bf[:], 0.0).then_inc(s_made, 1)
            pool.memset(causal[:], 0.0).then_inc(s_made, 1)
            pool.memset(half_pi[:], math.pi / 2).then_inc(s_made, 1)
            pool.memset(headsum[:], 1.0).then_inc(s_made, 1)
            pool.wait_ge(s_made, 5)
            for m in (ident, ident_bf):
                pool.affine_select(out=m[:], in_=m[:], compare_op=ALU.not_equal, fill=1.0, base=0,
                                   pattern=[[-1, P]], channel_multiplier=1).then_inc(s_made2, 1)
            pool.affine_select(out=causal[:], in_=causal[:], compare_op=ALU.is_ge, fill=NEG, base=0,
                               pattern=[[-1, P]], channel_multiplier=1).then_inc(s_made2, 1)
            pool.affine_select(out=headsum[:], in_=headsum[:], compare_op=ALU.is_ge, fill=0.0, base=0,
                               pattern=[[-PAIRS, 3]], channel_multiplier=1).then_inc(s_made2, 1)
            pool.wait_ge(s_made2, 4)
            pool.affine_select(out=headsum[:], in_=headsum[:], compare_op=ALU.is_ge, fill=0.0, base=PAIRS - 1,
                               pattern=[[PAIRS, 3]], channel_multiplier=-1).then_inc(s_made2, 1)
            with pool.Fori(0, NB) as b:
                pool.wait_ge(s_acc, (b + 1) * NE + START)
                pool.dma_start(rows(x1[bass.ds(b, 1), :, :].rearrange("a t d -> (a t) d")), xr[:]).then_inc(s_st1, 16)
                pool.wait_ge(s_st1, b * 16 + 16)
                pool.sem_inc(s_kept1, 1)
            with pool.Fori(0, NB) as b:
                pool.wait_ge(s_xdone[3], b + 1)
                pool.dma_start(rows(out[bass.ds(b, 1), :, :].rearrange("a t d -> (a t) d")), xr[:]).then_inc(s_st2, 16)
                pool.wait_ge(s_st2, b * 16 + 16)
                pool.sem_inc(s_kept2, 1)

        @block.scalar
        def _(sc):
            sc.sem_inc(s_e, START)
            sc.wait_ge(s_made2, 5)

            def layer_norm_copy(n, b):
                sc.wait_ge(s_hTp[n], b + 1)
                sc.activation(hT[:, 0, :], bank[0][:], ACT.Copy).then_inc(s_hTa[n], 1)

            with sc.Fori(0, NB) as b:
                layer_norm_copy(0, b)
                for hf in range(2):
                    for j, dst in enumerate((al, be, ge, go)):
                        sc.wait_ge(s_pa, b * 8 + hf * 4 + j + 1)
                        if j < 2:
                            sc.activation(dst[:, hf, :], bank[4 + j][0:HALF, :], ACT.Tanh, scale=0.5).then_inc(s_ga, 1)
                        else:
                            sc.activation(dst[:, hf, :], bank[4 + j][0:HALF, :], ACT.Silu).then_inc(s_ga, 1)
                    for j, dst in enumerate((al, be)):
                        sc.wait_ge(s_ga, b * 8 + hf * 4 + j + 1)
                        sc.activation(dst[:, hf, :], dst[:, hf, :], ACT.Copy, scale=0.5, bias=0.5
                                      ).then_inc(s_ab, 1)
                    sc.wait_ge(s_rng, b * 2 + hf + 1)
                    sc.activation(ab[:, hf, :], ang[:, hf, :], ACT.Abs).then_inc(s_abs, 1)
                    sc.activation(sn[:, hf, :], ang[:, hf, :], ACT.Sin)
                    sc.wait_ge(s_abs, b * 2 + hf + 1)
                    sc.activation(cs[:, hf, :], ab[:, hf, :], ACT.Sin, scale=-1.0, bias=half_pi[0:HALF, :]
                                  ).then_inc(s_trig, 1)
                for hf in range(2):
                    sc.wait_ge(s_scan, b * 2 + hf + 1)
                    sc.activation(sn[:, hf, :], oe[:, hf, :], ACT.Square)
                    sc.activation(cs[:, hf, :], oo[:, hf, :], ACT.Square).then_inc(s_sq, 1)
                layer_norm_copy(1, b)
                sc.wait_ge(s_lgc, b + 1)
                sc.activation(aff[:], bia[:], ACT.Exp, scale=-1.0).then_inc(s_ex, 1)

                for e in (0, 1):
                    sc.wait_ge(s_gu, b * NE + e + 1)
                    sc.activation(sg[e][:], bank[e][:], ACT.Silu).then_inc(s_silu, 1)
                with sc.Fori(2, NE, 2) as e:
                    for p in range(2):
                        sc.wait_ge(s_gu, b * NE + e + (p + 1))
                        sc.wait_ge(s_act, b * NE + e + (p - 1))
                        sc.activation(sg[p][:], bank[p][:], ACT.Silu).then_inc(s_silu, 1)

            with sc.Fori(0, NB) as b:
                layer_norm_copy(2, b)

                def copy_qk(g):
                    sc.wait_ge(s_q, g + 1)
                    sc.activation(qs[:], bank[0][:], ACT.Copy).then_inc(s_qe, 1)
                    sc.wait_ge(s_k, g + 1)
                    sc.activation(ks[:], bank[1][:], ACT.Copy).then_inc(s_ke, 1)

                def softmax(g):
                    sc.wait_ge(s_nb, g + 1)
                    for i in range(NT):
                        n = (i + 1) * P
                        ins = sc.activation(pr[:, i, 0:n], score(i), ACT.Exp, bias=nbias[:, i:i + 1], scale=SCALE,
                                            accum_out=rsum[:, i:i + 1])
                    ins.then_inc(s_e, 1)

                def copy_probs(g):
                    sc.wait_ge(s_t, g + 1)
                    sc.activation(pt[:, 0, :], bank[5][:], ACT.Copy)
                    sc.activation(pt[:, 2, 0:2 * P], bank[7][:, 0:2 * P], ACT.Copy).then_inc(s_ta, 1)

                copy_qk(b * NH)
                softmax(b * NH)
                with sc.Fori(0, NH - 1) as h:
                    copy_qk(b * NH + h + 1)
                    copy_probs(b * NH + h)
                    softmax(b * NH + h + 1)
                copy_probs(b * NH + NH - 1)
                layer_norm_copy(3, b)
                for m, (m0, mn) in enumerate(MT):
                    sc.wait_ge(s_fg, b * NM + m + 1)
                    if m >= 2:
                        sc.wait_ge(s_fa, b * NM + m - 1)
                    sc.activation(fsg[m % 2][0:mn, :], bank[m % 2][0:mn, :], ACT.Silu).then_inc(s_fs, 1)


        @block.vector
        def _(ve_):
            v = ve_
            for s in (s_x0free, s_x1free, s_acc, s_lut, s_ob):
                v.sem_inc(s, START)
            v.wait_ge(s_const, 16 * CONST_DMAS)
            v.memset(mask[:], SHARED_RATIO).then_inc(s_setup, 1)
            v.memset(fws[:], 0.0)
            for k in range(KD):
                for j in range(2):
                    v.tensor_copy(wabr[:, k, j].rearrange("p h (a c) -> p (h a) c", c=PAIRS),
                                  wabs[:, k, j, :].unsqueeze(2).to_broadcast([P, HEADS0, PAIRS]))
            v.tensor_scalar(cws[:, 0], cws[:, 0], invfs[:, 0:1], -1.0, ALU.mult, ALU.mult)
            v.tensor_scalar(cws[:, 1], cws[:, 1], invfs[:, 0:1], None, ALU.mult).then_inc(s_setup, 1)
            v.wait_ge(s_setup, 2)

            def rsqrt(n, link, extra):
                link(v.tensor_scalar(ry[:, 0:n].bitcast(I32), va[:, 0:n].bitcast(I32), -0.5, RSQRT_SEED,
                                     ALU.mult, ALU.add))
                for _ in range(3):
                    link(v.tensor_tensor(rt[:, 0:n], ry[:, 0:n], ry[:, 0:n], ALU.mult))
                    link(v.scalar_tensor_tensor(rt[:, 0:n], rt[:, 0:n], -0.5, va[:, 0:n], ALU.mult, ALU.mult))
                    link(v.scalar_tensor_tensor(ry[:, 0:n], rt[:, 0:n], 1.5, ry[:, 0:n], ALU.add, ALU.mult))

            def layer_norm(n, b, src):
                done = [0]

                def link(ins):
                    done[0] += 1
                    ins.then_inc(s_lnc[n], 1)
                    v.wait_ge(s_lnc[n], b * LN_LINKS + done[0])

                for i in range(NT):
                    ins = v.bn_stats(stats[:, i, :], src[:, i, :])
                link(ins)
                v.tensor_tensor(mv[:, :, 0], stats[:, :, 1], stats[:, :, 4], ALU.add)
                v.tensor_tensor(rt[:, 0:NT], stats[:, :, 1], stats[:, :, 4], ALU.subtract)
                link(v.tensor_tensor(mv[:, :, 1], stats[:, :, 2], stats[:, :, 5], ALU.add))
                v.tensor_scalar(mv[:, :, 0], mv[:, :, 0], 0.5, None, ALU.mult)
                v.tensor_scalar(mv[:, :, 1], mv[:, :, 1], 1.0 / D, EPS, ALU.mult, ALU.add)
                link(v.tensor_tensor(rt[:, 0:NT], rt[:, 0:NT], rt[:, 0:NT], ALU.mult))
                link(v.scalar_tensor_tensor(va[:, 0:NT], rt[:, 0:NT], 0.25, mv[:, :, 1], ALU.mult, ALU.add))
                rsqrt(NT, link, 0)
                assert done[0] == LN_LINKS
                for i in range(NT):
                    ins = v.tensor_scalar(xn[:, i, :], src[:, i, :], mv[:, i, 0:1], ry[:, i:i + 1],
                                          ALU.subtract, ALU.mult)
                ins.then_inc(s_xn[n], 1)
                v.wait_ge(s_hTp[n], b + 1)
                v.tensor_copy(hT[:, 1, :], bank[1][:]).then_inc(s_hTv[n], 1)

            with v.Fori(0, NB) as b:
                v.wait_ge(s_x0, (b + 1) * 16)
                layer_norm(0, b, xin)
                done = [0]

                def link(ins):
                    done[0] += 1
                    ins.then_inc(s_l0, 1)
                    v.wait_ge(s_l0, b * L0_LINKS + done[0])

                def conv_tile(n, dst, hf, quant, first):
                    v.wait_ge(s_pv, b * 8 + n + 1)
                    src = bank[n % 4][0:HALF, :]
                    tap = [cws[:, quant, hf, j:j + 1] for j in range(TAPS)]
                    d = dst[:, hf, :]
                    if first:
                        link(v.tensor_scalar(d, src, tap[TAPS - 1], None, ALU.mult))
                    else:
                        link(v.scalar_tensor_tensor(d, src, tap[TAPS - 1], d, ALU.mult, ALU.add))
                    for s in range(1, TAPS):
                        ins = v.scalar_tensor_tensor(d[:, s:T], src[:, 0:T - s], tap[TAPS - 1 - s], d[:, s:T],
                                                     ALU.mult, ALU.add)
                        if s < TAPS - 1:
                            link(ins)
                    ins.then_inc(s_cv, 1)
                    v.wait_ge(s_cv, b * 8 + n + 1)

                for hf in range(2):
                    conv_tile(4 * hf + 0, ang, hf, 0, True)
                    conv_tile(4 * hf + 1, ang, hf, 1, False)
                    a, n_ = ang[:, hf, :], turns[:, hf, :]
                    link(v.tensor_scalar(n_, a, 1.0 / TWO_PI, ROUND, ALU.mult, ALU.add))
                    link(v.tensor_scalar(n_, n_, ROUND, None, ALU.subtract))
                    link(v.scalar_tensor_tensor(a, n_, -PI_HI, a, ALU.mult, ALU.add))
                    link(v.scalar_tensor_tensor(a, n_, -PI_LO, a, ALU.mult, ALU.add))
                    v.tensor_scalar(a, a, PI_MAX, -PI_MAX, ALU.min, ALU.max).then_inc(s_rng, 1)
                    conv_tile(4 * hf + 2, ve, hf, 2, True)
                    conv_tile(4 * hf + 3, vo, hf, 3, True)
                for hf in range(2):
                    v.wait_ge(s_trig, b * 2 + hf + 1)
                    v.wait_ge(s_ab, b * 4 + 2 * hf + 2)
                    h = (slice(None), hf, slice(None))
                    v.tensor_tensor(cs[h], cs[h], be[h], ALU.mult)
                    link(v.tensor_tensor(sn[h], sn[h], be[h], ALU.mult))
                    v.tensor_tensor(t1[h], ve[h], cs[h], ALU.mult)
                    v.tensor_tensor(t2[h], vo[h], sn[h], ALU.mult)
                    v.tensor_tensor(t3[h], vo[h], cs[h], ALU.mult)
                    link(v.tensor_tensor(t4[h], ve[h], sn[h], ALU.mult))
                    v.tensor_tensor(t1[h], t1[h], t2[h], ALU.subtract)
                    link(v.tensor_tensor(t3[h], t3[h], t4[h], ALU.add))
                    v.tensor_tensor_scan(oe[h], al[h], t1[h], 0.0, ALU.mult, ALU.add)
                    v.tensor_tensor_scan(oo[h], al[h], t3[h], 0.0, ALU.mult, ALU.add).then_inc(s_scan, 1)
                v.wait_ge(s_scan, b * 2 + 2)
                v.wait_ge(s_ga, b * 8 + 8)
                for hf in range(2):
                    h = (slice(None), hf, slice(None))
                    v.scalar_tensor_tensor(ge[h], ge[h], rmsws[:, 0:1], oe[h], ALU.mult, ALU.mult)
                    ins = v.scalar_tensor_tensor(go[h], go[h], rmsws[:, 1:2], oo[h], ALU.mult, ALU.mult)
                link(ins)
                v.wait_ge(s_ms, b + 1)
                link(v.tensor_scalar(va[:], bank[2][:, 0:NT * HEADS0], 1.0 / (2 * PAIRS), EPS, ALU.mult, ALU.add))
                rsqrt(NT * HEADS0, link, 0)
                v.tensor_copy(rexp[:].rearrange("p t h c -> p (t h) c"),
                              ry[:].unsqueeze(2).to_broadcast([P, NT * HEADS0, PAIRS])).then_inc(s_re, 1)
                v.wait_ge(s_rT, b + 1)
                for hf in range(2):
                    h = (slice(None), hf, slice(None))
                    v.tensor_tensor(ge[h], ge[h], bank[4 + hf][0:HALF, :], ALU.mult)
                    ins = v.tensor_tensor(go[h], go[h], bank[4 + hf][0:HALF, :], ALU.mult)
                ins.then_inc(s_y, 1)
                assert done[0] == L0_LINKS, done[0]
                v.wait_ge(s_o0, b + 1)
                v.wait_ge(s_kept1, b + START)
                for i in range(2):
                    ins = v.tensor_tensor(xr[:, 2 * i:2 * i + 2, :].rearrange("p n d -> p (n d)"), bank[6 + i][:],
                                          xin[:, 2 * i:2 * i + 2, :].rearrange("p n d -> p (n d)"), ALU.add)
                ins.then_inc(s_x0free, 1)
                v.wait_ge(s_x0free, b + 1 + START)

                layer_norm(1, b, xr)
                rdone = [0]

                def rlink(ins):
                    rdone[0] += 1
                    ins.then_inc(s_rc, 1)
                    v.wait_ge(s_rc, b * RC_LINKS + rdone[0])

                v.wait_ge(s_lg, b + 1)
                v.tensor_scalar(bia[:], bank[2][:, 0:NT * NEXP].rearrange("p (t e) -> p t e", t=NT), -87.0, None,
                                ALU.max).then_inc(s_lgc, 1)
                v.wait_ge(s_ex, b + 1)
                rlink(v.tensor_scalar(r1[:], aff[:], 1.0, None, ALU.add))
                rlink(v.reciprocal(aff[:], r1[:]))
                rlink(v.tensor_tensor(bia[:], aff[:], gbiass[:], ALU.add))
                for turn in range(2):
                    rlink(v.tensor_reduce(m1[:], bia[:], AX_X, ALU.max))
                    rlink(v.tensor_tensor(r1[:], bia[:], m1[:].unsqueeze(2).to_broadcast([P, NT, NEXP]), ALU.is_lt))
                    rlink(v.scalar_tensor_tensor(r1[:].rearrange("p t e -> p (t e)"),
                                                 r1[:].rearrange("p t e -> p (t e)"), float(NE),
                                                 iotas[:].rearrange("p t e -> p (t e)"), ALU.mult, ALU.add))
                    rlink(v.tensor_reduce(m1[:], r1[:], AX_X, ALU.min))
                    dst = pick if turn == 0 else r2
                    rlink(v.tensor_tensor(dst[:], iotas[:], m1[:].unsqueeze(2).to_broadcast([P, NT, NEXP]),
                                          ALU.is_equal))
                    if turn == 0:
                        rlink(v.scalar_tensor_tensor(bia[:].rearrange("p t e -> p (t e)"),
                                                     pick[:].rearrange("p t e -> p (t e)"), -3.0e38,
                                                     bia[:].rearrange("p t e -> p (t e)"), ALU.mult, ALU.add))
                rlink(v.tensor_tensor(pick[:], pick[:], r2[:], ALU.add))
                rlink(v.tensor_tensor(pick[:], pick[:], aff[:], ALU.mult))
                rlink(v.tensor_reduce(m1[:], pick[:], AX_X, ALU.add))
                rlink(v.tensor_scalar(m1[:], m1[:], 1e-9, None, ALU.add))
                rlink(v.reciprocal(m1[:], m1[:]))
                assert rdone[0] == RC_LINKS, rdone[0]
                v.tensor_tensor(mask[:, :, 0:NEXP], pick[:], m1[:].unsqueeze(2).to_broadcast([P, NT, NEXP]),
                                ALU.mult).then_inc(s_mask, 1)
                v.wait_ge(s_mask, b + 1)

                def activate(g, p):
                    v.wait_ge(s_silu, g + 1)
                    v.wait_ge(s_up, g + 1)
                    v.tensor_tensor(act[p][:], sg[p][:], bank[2 + p][:], ALU.mult).then_inc(s_act, 1)

                def accumulate(g, e, p):
                    v.wait_ge(s_dn, g + 1 + START)
                    v.wait_ge(s_acc, g + START)
                    for i in range(NT):
                        ins = v.scalar_tensor_tensor(xr[:, i, :], bank[4 + 2 * p + i // 2][:, (i % 2) * D:(i % 2 + 1) * D],
                                                     mask[:, i, bass.ds(e, 1)], xr[:, i, :], ALU.mult, ALU.add)
                    ins.then_inc(s_acc, 1)

                def lut_step(g, e):
                    v.tensor_scalar(ftmp[:], fidxs[:, bass.ds(b * LC, LC)], lutks[:, bass.ds(e, 1)],
                                    luts[:, bass.ds(e, 1)], ALU.is_equal, ALU.mult).then_inc(s_lut, 1)
                    v.wait_ge(s_lut, 2 * g + 1 + START)
                    v.tensor_tensor(fws[:, bass.ds(b * LC, LC)], fws[:, bass.ds(b * LC, LC)], ftmp[:],
                                    ALU.add).then_inc(s_lut, 1)

                activate(b * NE, 0)
                with v.Fori(0, NE - 2, 2) as e:
                    for p in range(2):
                        g = b * NE + e + p
                        v.wait_ge(s_lut, 2 * g + START)
                        lut_step(g, e + p)
                        activate(g + 1, 1 - p)
                        accumulate(g, e + p, p)
                activate(b * NE + NE - 1, 1)
                accumulate(b * NE + NE - 2, NE - 2, 0)
                accumulate(b * NE + NE - 1, NE - 1, 1)
                for e in (NE - 2, NE - 1):
                    v.wait_ge(s_lut, 2 * (b * NE + e) + START)
                    lut_step(b * NE + e, e)

            with v.Fori(0, NB) as b:
                v.wait_ge(s_x1, (b + 1) * 16)
                layer_norm(2, b, xin)
                v.wait_ge(s_kept2, b + START)
                v.tensor_copy(xr[:], xin[:]).then_inc(s_x1free, 1)
                v.wait_ge(s_x1free, b + 1 + START)

                def copy_v(g, p):
                    v.wait_ge(s_v, g + 1)
                    v.tensor_copy(vs[p][:].rearrange("p t n -> p (t n)"), bank[0][:]).then_inc(s_ve, 1)

                def score_max(g):
                    v.wait_ge(s_s, g + 1)
                    for i in range(NT):
                        ins = v.tensor_reduce(mx[:, i:i + 1], score(i), AX_X, ALU.max)
                    ins.then_inc(s_mx, 1)
                    v.wait_ge(s_mx, g + 1)
                    v.tensor_scalar(nbias[:], mx[:], -SCALE, None, ALU.mult).then_inc(s_nb, 1)

                def copy_probs_z(g):
                    v.wait_ge(s_t, g + 1)
                    v.tensor_copy(pt[:, 1, :], bank[6][:]).then_inc(s_tv, 1)
                    v.wait_ge(s_z, g + 1)
                    v.tensor_copy(zs[:], bank[1][:]).then_inc(s_ze, 1)
                    v.wait_ge(s_ob, g + START)
                    v.reciprocal(rinv[:], rsum[:]).then_inc(s_ri, 1)

                def add_out(g):
                    v.wait_ge(s_o, g + 1 + START)
                    v.wait_ge(s_ri, g + 1)
                    v.wait_ge(s_ob, g + START)
                    for i in range(NT):
                        ins = v.scalar_tensor_tensor(xr[:, i, :], bank[i // 2][:, (i % 2) * D:(i % 2 + 1) * D],
                                                     rinv[:, i:i + 1], xr[:, i, :], ALU.mult, ALU.add)
                    ins.then_inc(s_ob, 1)

                copy_v(b * NH, 0)
                score_max(b * NH)
                with v.Fori(0, NH - 2, 2) as h:
                    for p in range(2):
                        g = b * NH + h + p
                        copy_v(g + 1, 1 - p)
                        copy_probs_z(g)
                        score_max(g + 1)
                        add_out(g)
                copy_v(b * NH + NH - 1, 1)
                copy_probs_z(b * NH + NH - 2)
                score_max(b * NH + NH - 1)
                add_out(b * NH + NH - 2)
                copy_probs_z(b * NH + NH - 1)
                add_out(b * NH + NH - 1)
                v.wait_ge(s_ob, b * NH + NH + START)
                layer_norm(3, b, xr)
                for m, (m0, mn) in enumerate(MT):
                    v.wait_ge(s_fs, b * NM + m + 1)
                    v.wait_ge(s_fu, b * NM + m + 1)
                    v.tensor_tensor(fa[0:mn, m, :], fsg[m % 2][0:mn, :], bank[2 + m % 2][0:mn, :], ALU.mult
                                    ).then_inc(s_fa, 1)
                v.wait_ge(s_fd, b + 1)
                for i in range(2):
                    x2 = xr[:, 2 * i:2 * i + 2, :].rearrange("p n d -> p (n d)")
                    ins = v.tensor_tensor(x2, bank[4 + i][:], x2, ALU.add)
                ins.then_inc(s_xdone[3], 1)


        @block.tensor
        def _(pe):
            mm = pe.matmul
            for s in (s_dn, s_o):
                pe.sem_inc(s, START)
            pe.wait_ge(s_const, 16 * CONST_DMAS)
            pe.wait_ge(s_made2, 5)
            pe.wait_ge(s_setup, 2)

            def layer_norm_transpose(n, b):
                pe.wait_ge(s_xn[n], b + 1)
                for k in range(KD):
                    for i in range(NT):
                        ins = pe.transpose(bank[k][:, i * P:(i + 1) * P], xn[:, i, k * P:(k + 1) * P], ident[:])
                ins.then_inc(s_hTp[n], 1)
                pe.wait_ge(s_hTa[n], b + 1)
                pe.wait_ge(s_hTv[n], b + 1)

            def project(dst, w):
                for k in range(KD):
                    ins = mm(dst, w(k), hT[:, k, :], start=(k == 0), stop=(k == KD - 1))
                return ins

            with pe.Fori(0, NB) as b:
                layer_norm_transpose(0, b)
                for hf in range(2):
                    def w_of(q):
                        return lambda k: w0s[:, k, q, hf, :]

                    def ab_of(j):
                        return lambda k: wabr[:, k, j, hf, :]

                    plan = [("v", 0, w_of(0)), ("v", 1, w_of(1)), ("a", 0, ab_of(0)), ("a", 1, ab_of(1)),
                            ("v", 2, w_of(2)), ("v", 3, w_of(3)), ("a", 2, w_of(4)), ("a", 3, w_of(5))]
                    for kind, j, w in plan:
                        if hf == 1:
                            pe.wait_ge(s_cv if kind == "v" else s_ga, b * 8 + j + 1)
                        dst = bank[j if kind == "v" else 4 + j][0:HALF, :]
                        project(dst, w).then_inc(s_pv if kind == "v" else s_pa, 1)
                pe.wait_ge(s_cv, b * 8 + 8)
                for hf in range(2):
                    pe.wait_ge(s_sq, b * 2 + hf + 1)
                    for i in range(NT):
                        dst = bank[2][:, i * HEADS0 + 3 * hf:i * HEADS0 + 3 * hf + 3]
                        mm(dst, sn[:, hf, i * P:(i + 1) * P], headsum[:], start=True, stop=False)
                        ins = mm(dst, cs[:, hf, i * P:(i + 1) * P], headsum[:], start=False, stop=True)
                ins.then_inc(s_ms, 1)
                pe.wait_ge(s_re, b + 1)
                pe.wait_ge(s_ga, b * 8 + 8)
                for hf in range(2):
                    for i in range(NT):
                        ins = pe.transpose(bank[4 + hf][0:HALF, i * P:(i + 1) * P],
                                           rexp[:, i, 3 * hf:3 * hf + 3, :].rearrange("p h c -> p (h c)"), ident[:])
                ins.then_inc(s_rT, 1)
                pe.wait_ge(s_y, b + 1)
                for i in range(NT):
                    dst = bank[6 + i // 2][:, (i % 2) * D:(i % 2 + 1) * D]
                    n = 0
                    for hf in range(2):
                        for par, src in enumerate((ge, go)):
                            ins = mm(dst, src[:, hf, i * P:(i + 1) * P], wo0s[:, hf, par, :], start=(n == 0),
                                     stop=(n == 3))
                            n += 1
                ins.then_inc(s_o0, 1)

                layer_norm_transpose(1, b)
                for i in range(NT):
                    for k in range(KD):
                        ins = mm(bank[2][:, i * NEXP:(i + 1) * NEXP], hT[:, k, i * P:(i + 1) * P], cents[:, k, :],
                                 start=(k == 0), stop=(k == KD - 1))
                ins.then_inc(s_lg, 1)

                def gate_up(g, p, nload):
                    pe.wait_ge(s_w[p], nload * 16)
                    pe.wait_ge(s_silu, g - 1)
                    project(bank[p][:], lambda k: we[p][:, k * P:(k + 1) * P]).then_inc(s_gu, 1)
                    pe.wait_ge(s_act, g - 1)
                    project(bank[2 + p][:], lambda k: we[p][:, D + k * P:D + (k + 1) * P]).then_inc(s_up, 1)

                def gate_up_first(g, p, nload):
                    pe.wait_ge(s_w[p], nload * 16)
                    pe.wait_ge(s_lgc, b + 1)
                    project(bank[p][:], lambda k: we[p][:, k * P:(k + 1) * P]).then_inc(s_gu, 1)
                    project(bank[2 + p][:], lambda k: we[p][:, D + k * P:D + (k + 1) * P]).then_inc(s_up, 1)

                def down(g, p):
                    pe.wait_ge(s_act, g + 1)
                    for i in range(NT):
                        ins = mm(bank[4 + 2 * p + i // 2][:, (i % 2) * D:(i % 2 + 1) * D],
                                 act[p][:, i * P:(i + 1) * P], we[p][:, 2 * D:3 * D], start=True, stop=True)
                    ins.then_inc(s_dn, 1)

                gate_up_first(b * NE, 0, b * (NE // 2) + 1)
                gate_up_first(b * NE + 1, 1, b * (NE // 2) + 1)
                down(b * NE, 0)
                with pe.Fori(0, NE // 2 - 1) as i:
                    for p in (1, 0):
                        g = b * NE + 2 * i + (2 - p)
                        gate_up(g + 1, 1 - p, b * (NE // 2) + i + 2)
                        pe.wait_ge(s_acc, g - 1 + START)
                        down(g, p)
                pe.wait_ge(s_acc, b * NE + NE - 2 + START)
                down(b * NE + NE - 1, 1)

            with pe.Fori(0, NB) as b:
                layer_norm_transpose(2, b)

                def qkv(g, p, nload):
                    pe.wait_ge(s_wh[p], nload * 16)
                    project(bank[0][:], lambda k: wh[p][:, 0, k, :]).then_inc(s_q, 1)
                    project(bank[1][:], lambda k: wh[p][:, 1, k, :]).then_inc(s_k, 1)
                    pe.wait_ge(s_qe, g + 1)
                    for i in range(NT):
                        for k in range(KD):
                            ins = mm(bank[0][:, i * P:(i + 1) * P], hT[:, k, i * P:(i + 1) * P], wh[p][:, 2, k, :],
                                     start=(k == 0), stop=(k == KD - 1))
                    ins.then_inc(s_v, 1)

                def scores(g):
                    pe.wait_ge(s_ke, g + 1)
                    pe.wait_ge(s_e, g + START)
                    for i in range(NT):
                        n = (i + 1) * P
                        dst = score(i)
                        mm(dst, qs[:, i * P:(i + 1) * P], ks[:, 0:n], start=True, stop=False)
                        ins = mm(dst[:, i * P:n], ident_bf[:], causal[:], start=False, stop=True)
                    ins.then_inc(s_s, 1)

                def transpose_probs(g):
                    pe.wait_ge(s_e, g + 1 + START)
                    for j in range(NT):
                        for i in range(j, NT):
                            dst = bank[5 + (1 if j == 3 else j)]
                            c = 3 * P if j == 3 else (i - j) * P
                            ins = pe.transpose(dst[:, c:c + P], pr[:, i, j * P:(j + 1) * P], ident[:])
                    ins.then_inc(s_t, 1)

                def zed(g, p):
                    pe.wait_ge(s_ta, g + 1)
                    pe.wait_ge(s_tv, g + 1)
                    src = [pt[:, 0, 0:T], pt[:, 1, 0:3 * P], pt[:, 2, 0:2 * P], pt[:, 1, 3 * P:T]]
                    for j in range(NT):
                        ins = mm(bank[1][:, j * P:T], vs[p][:, j, :], src[j], start=(j == 0), stop=(j == NT - 1))
                    ins.then_inc(s_z, 1)

                def project_out(g, p, nload):
                    pe.wait_ge(s_wo[p], nload * 16)
                    pe.wait_ge(s_ze, g + 1)
                    for i in range(NT):
                        ins = mm(bank[i // 2][:, (i % 2) * D:(i % 2 + 1) * D], zs[:, i * P:(i + 1) * P], who[p][:],
                                 start=True, stop=True)
                    ins.then_inc(s_o, 1)

                qkv(b * NH, 0, b * (NH // 2) + 1)
                scores(b * NH)

                def head(h, p, n, last=False):
                    g = b * NH + h
                    if not last:
                        pe.wait_ge(s_ob, g + START)
                        pe.wait_ge(s_ve, g + 1)
                        qkv(g + 1, 1 - p, n + (1 if p else 0))
                        pe.wait_ge(s_ve, g + 2)
                        pe.wait_ge(s_ke, g + 2)
                    transpose_probs(g)
                    zed(g, p)
                    if not last:
                        scores(g + 1)
                    project_out(g, p, n)

                with pe.Fori(0, NH // 2 - 1) as i:
                    for p in range(2):
                        head(2 * i + p, p, b * (NH // 2) + i + 1)
                head(NH - 2, 0, b * (NH // 2) + NH // 2)
                head(NH - 1, 1, b * (NH // 2) + NH // 2, last=True)

                layer_norm_transpose(3, b)
                for m, (m0, mn) in enumerate(MT):
                    if m >= 2:
                        pe.wait_ge(s_fs, b * NM + m - 1)
                    project(bank[m % 2][0:mn, :], lambda k: f_gate[:, k, m0:m0 + mn]).then_inc(s_fg, 1)
                    if m >= 2:
                        pe.wait_ge(s_fa, b * NM + m - 1)
                    project(bank[2 + m % 2][0:mn, :], lambda k: f_up[:, k, m0:m0 + mn]).then_inc(s_fu, 1)
                pe.wait_ge(s_fa, b * NM + NM)
                for i in range(NT):
                    for m, (m0, mn) in enumerate(MT):
                        ins = mm(bank[4 + i // 2][:, (i % 2) * D:(i % 2 + 1) * D], fa[0:mn, m, i * P:(i + 1) * P],
                                 f_down[0:mn, m, :], start=(m == 0), stop=(m == NM - 1))
                ins.then_inc(s_fd, 1)


_OUT = (NB, T, D)


def kernel(**inputs):
    import concourse.bacc as bacc
    from concourse.bass_utils import run_bass_kernel_spmd

    a = {k: np.asarray(v) for k, v in inputs.items()}

    def halves(w, parity):
        return w[..., parity::2].reshape(*w.shape[:-1], 2, HALF)

    def kt(w):
        return w.reshape(KD, P, -1).transpose(1, 0, 2)

    wq, wk, wv, wg = (a["L0_attn_W" + c] for c in "qkvg")
    w0 = np.stack([halves(wq, 0), halves(wk, 0), halves(wv, 0), halves(wv, 1), halves(wg, 0), halves(wg, 1)], 1)
    w0 = kt(w0.reshape(D, -1)).reshape(P, KD, 6, 2, HALF)
    wab = kt(np.concatenate([a["L0_attn_Wa"], a["L0_attn_Wb"]], 1)).reshape(P, KD, 2, HEADS0)
    cq, ck, cv = (a["L0_attn_conv_" + c].T for c in "qkv")
    cw = np.stack([halves(cq, 0), halves(ck, 0), halves(cv, 0), halves(cv, 1)])
    cw = cw.transpose(3, 0, 2, 1)
    invf = np.tile((1.0 / 10000.0 ** (np.arange(0, 64, 2, dtype=np.float32) / np.float32(64))).astype(np.float32), 3)
    rw = np.tile(a["L0_attn_rms_w"].reshape(PAIRS, 2), (3, 1))
    wo0 = a["L0_attn_Wo"].reshape(2, HALF, 2, D).transpose(1, 0, 2, 3)
    cent = kt(a["L0_ffn_centroids"].T)
    gb = np.tile(a["L0_ffn_gate_bias"], (P, NT, 1))
    gate = np.concatenate([a["L0_ffn_wg"], a["L0_ffn_wg_s"].reshape(D, NSHARED, P).transpose(1, 0, 2)])
    up = np.concatenate([a["L0_ffn_wu"], a["L0_ffn_wu_s"].reshape(D, NSHARED, P).transpose(1, 0, 2)])
    down = np.concatenate([a["L0_ffn_wd"], a["L0_ffn_wd_s"].reshape(NSHARED, P, D)])

    def ekt(w):
        return w.reshape(NE, KD, P, P).transpose(0, 2, 1, 3).reshape(NE, P, D)

    wexp = np.concatenate([ekt(gate), ekt(up), down], 2)
    iota = np.tile(np.arange(NEXP, dtype=np.float32), (P, NT, 1))
    lutk = np.tile(np.arange(NE, dtype=np.float32), (P, 1))
    qkv = np.stack([a["L1_attn_W_Q"], a["L1_attn_W_K"], a["L1_attn_W_V"]], 1)
    qkv = qkv.reshape(NH, 3, DH, KD, P).transpose(0, 4, 1, 3, 2).reshape(NH, P, -1)
    wo1 = a["L1_attn_W_O"].reshape(D, NH, DH).transpose(1, 2, 0)
    gi, ui, di = (a[f"L1_ffn_{n}_idx"] for n in ("gate", "up", "down"))
    dpad = np.zeros((NM * P, D), di.dtype)
    dpad[:INTER] = di.T
    fidx = np.concatenate([kt(gi.T).reshape(P, -1), kt(ui.T).reshape(P, -1),
                           dpad.reshape(NM, P, D).transpose(1, 0, 2).reshape(P, -1)], 1)
    lut = np.zeros((P, NE), np.float32)
    lut[:, :LUTN] = a["L1_ffn_lut"]

    named = dict(x=a["L0_attn_hidden_states"], w0=w0, wab=wab, cw=cw, invf=invf[:, None], rmsw=rw, wo0=wo0, cent=cent,
                 gbias=gb, wexp=wexp, iota=iota, lutk=lutk, wqkv=qkv, wo1=wo1, fidx=fidx, lut=lut)
    nc = bacc.Bacc("TRN2", target_bir_lowering=False, num_devices=1)
    arrays, args = {}, []
    for name, arr in named.items():
        arr = np.ascontiguousarray(arr)
        arrays[f"in_{name}"] = arr
        args.append(nc.dram_tensor(f"in_{name}", arr.shape, mybir.dt.from_np(arr.dtype), kind="ExternalInput").ap())
    args.append(nc.dram_tensor("out_x", _OUT, F32, kind="ExternalOutput").ap())
    two_layer_program(nc, *args)
    r = run_bass_kernel_spmd(nc, [arrays], core_ids=[0])
    return r.results[0]["out_x"]
```

```python
from contextlib import ExitStack
import math

import numpy as np
import concourse.bass as bass
from concourse import mybir

ALU = mybir.AluOpType
ACT = mybir.ActivationFunctionType
F32 = mybir.dt.float32
F32R = mybir.dt.float32r
BF16 = mybir.dt.bfloat16
I32 = mybir.dt.int32
AX_X = mybir.AxisListType.X

P = 128
NB, T, D = 8, 512, 256
NT = T // P
KD = D // P
HEADS0, PAIRS = 6, 32
HALF = HEADS0 * PAIRS // 2
TAPS = 4
EPS = 1e-5
NEXP, NSHARED = 16, 2
NE = NEXP + NSHARED
SHARED_RATIO = 0.1
NH, DH = 16, 128
SCALE = 1.0 / math.sqrt(DH)
NEG = -1e10
INTER = 688
INTER_PAD = -(-INTER // P) * P
NM = INTER_PAD // P
LUTN = 16
FW = KD * INTER_PAD * 2 + NM * D
LC = FW // NB

TWO_PI = 2 * math.pi
ROUND = 1.5 * 2.0 ** 23
PI_HI = 6.28125
PI_LO = TWO_PI - PI_HI
PI_MAX = 3.1415925
RSQRT_SEED = float(0x5F3759DF)
START = 1
LN_LINKS = 14
L0_LINKS = 50
RC_LINKS = 19


def two_layer_program(nc, x_in, w0, wab, cw, invf, rmsw, wo0, cent, gbias, wexp, iota16, lutk, wqkvo, fidx, lut, out):
    ctx = ExitStack()
    with ctx:
        def sb(name, shape, dt=F32):
            return ctx.enter_context(nc.sbuf_tensor(name, shape, dt))

        def sem(name):
            return ctx.enter_context(nc.semaphore(name))

        x1 = nc.dram_tensor("x1_between_stages", [NB, T, D], F32, kind="Internal").ap()
        bank = [ctx.enter_context(nc.psum_tensor(f"bank{i}", [P, 512], F32)) for i in range(8)]

        ident = sb("ident", [P, P])
        ident_bf = sb("ident_bf", [P, P], BF16)
        causal = sb("causal", [P, P], BF16)
        half_pi = sb("half_pi", [P, 1])
        fws = sb("fws", [P, FW])
        xin = sb("xin", [P, NT, D])
        xr = sb("xr", [P, NT, D])
        xn = sb("xn", [P, NT, D])
        stats = sb("stats", [P, NT, 6])
        mv = sb("mv", [P, NT, 2])
        va = sb("va", [P, NT * HEADS0])
        ry = sb("ry", [P, NT * HEADS0])
        rt = sb("rt", [P, NT * HEADS0])

        stage1 = ExitStack()

        def sb1(name, shape, dt=F32):
            return stage1.enter_context(nc.sbuf_tensor(name, shape, dt))

        hT = sb1("hT", [P, KD, T])
        headsum = sb1("headsum", [HALF, 3])
        w0s = sb1("w0s", [P, KD, 6, 2, HALF])
        wabs = sb1("wabs", [P, KD, 2, HEADS0])
        wabr = sb1("wabr", [P, KD, 2, 2, HALF])
        cws = sb1("cws", [HALF, 4, 2, TAPS])
        invfs = sb1("invfs", [HALF, 1])
        rmsws = sb1("rmsws", [HALF, 2])
        wo0s = sb1("wo0s", [HALF, 2, 2, D])
        cents = sb1("cents", [P, KD, NEXP])
        gbiass = sb1("gbiass", [P, NT, NEXP])
        iotas = sb1("iotas", [P, NT, NEXP])
        lutks = sb1("lutks", [P, NE])
        luts = sb1("luts", [P, NE])
        fidxs = sb1("fidxs", [P, FW], I32)
        ftmp = sb1("ftmp", [P, LC])
        ang, turns, ve, vo, al, be, ge, go, sn, cs, t1, t2, t3, t4, oe, oo = (
            sb1(name, [HALF, 2, T]) for name in ("ang", "turns", "ve", "vo", "al", "be", "ge", "go", "sn", "cs",
                                                 "t1", "t2", "t3", "t4", "oe", "oo"))
        ab = turns
        rexp = sb1("rexp", [P, NT, HEADS0, PAIRS])
        wgu = [sb1(f"wgu{i}", [P, 2 * D]) for i in range(2)]
        wdn = [sb1(f"wdn{i}", [P, D]) for i in range(2)]
        aff = sb1("aff", [P, NT, NEXP])
        bia = sb1("bia", [P, NT, NEXP])
        r1 = sb1("r1", [P, NT, NEXP])
        r2 = sb1("r2", [P, NT, NEXP])
        m1 = sb1("m1", [P, NT])
        pick = sb1("pick", [P, NT, NEXP])
        mask = sb1("mask", [P, NT, NE])
        sg = [sb1(f"sg{i}", [P, T]) for i in range(2)]
        act = [sb1(f"act{i}", [P, T]) for i in range(2)]
        stage1.close()

        def split(name, shape):
            return [sb(f"{name}_{part}", shape, F32R) for part in ("high", "low")]

        fw2 = split("fw2", [P, FW])
        h2 = split("h2", [P, KD, T])
        wraw = [sb(f"wraw{i}", [P, 4 * D]) for i in range(2)]
        wqkv2 = [split(f"wqkv{i}", [P, 3, KD, DH]) for i in range(2)]
        wo2 = [split(f"wo{i}", [P, D]) for i in range(2)]
        q2 = split("q2", [P, T])
        k2 = split("k2", [P, T])
        v2 = [split(f"v2{i}", [P, NT, DH]) for i in range(2)]
        pr = sb("pr", [P, NT, T])
        p2 = split("p2", [P, 3, T])
        z2 = split("z2", [P, T])
        negmax = sb("negmax", [P, NT])
        rsum = sb("rsum", [P, NT])
        rinv = sb("rinv", [P, NT])
        fsg = [sb(f"fsg{i}", [P, T]) for i in range(2)]
        ft = [sb(f"ft{i}", [P, T]) for i in range(2)]
        fa2 = split("fa2", [P, NM, T])

        def ffn_weights(part):
            w = fw2[part]
            return (w[:, 0:KD * INTER_PAD].rearrange("p (k n) -> p k n", k=KD),
                    w[:, KD * INTER_PAD:2 * KD * INTER_PAD].rearrange("p (k n) -> p k n", k=KD),
                    w[:, 2 * KD * INTER_PAD:].rearrange("p (m n) -> p m n", m=NM))

        s_const = sem("consts_loaded")
        s_made = sem("consts_made")
        s_made2 = sem("consts_selected")
        s_setup = sem("setup_by_vector")
        s_set = sem("setup_chain")
        s_x0 = sem("x_loaded_stage1")
        s_x0free = sem("x_taken_stage1")
        s_x1 = sem("x_loaded_stage2")
        s_x1free = sem("x_taken_stage2")
        s_st1 = sem("x1_stored")
        s_st2 = sem("out_stored")
        s_kept1 = sem("residual_stored_stage1")
        s_xn = [sem(f"ln{n}_normalised") for n in range(4)]
        s_hTp = [sem(f"ln{n}_transposed") for n in range(4)]
        s_hTa = [sem(f"ln{n}_copied_by_scalar") for n in range(4)]
        s_hTv = [sem(f"ln{n}_copied_by_vector") for n in range(4)]
        s_lnc = [sem(f"ln{n}_chain") for n in range(4)]
        s_xdone = [sem(f"sublayer{n}_added") for n in range(4)]
        s_pv = sem("l0_projected_for_vector")
        s_pa = sem("l0_projected_for_scalar")
        s_cv = sem("l0_conv_done")
        s_ga = sem("l0_gates_read")
        s_gate = sem("l0_alpha_beta_tanh")
        s_ab = sem("l0_alpha_beta")
        s_rng = sem("l0_angle_reduced")
        s_abs = sem("l0_angle_abs")
        s_trig = sem("l0_sin_cos")
        s_scan = sem("l0_scanned")
        s_sq = sem("l0_squares")
        s_ms = sem("l0_square_sums")
        s_re = sem("l0_rms_spread")
        s_rT = sem("l0_rms_transposed")
        s_y = sem("l0_gated")
        s_o0 = sem("l0_out_product")
        s_l0 = sem("l0_chain")
        s_lg = sem("router_logits")
        s_lgc = sem("router_logits_clamped")
        s_ex = sem("router_exp")
        s_mask = sem("router_mask")
        s_rc = sem("router_chain")
        s_w = [sem(f"expert_gate_up_weights{i}") for i in range(2)]
        s_wd = [sem(f"expert_down_weights{i}") for i in range(2)]
        s_gu = sem("expert_gate_product")
        s_up = sem("expert_up_product")
        s_silu = sem("expert_silu")
        s_act = sem("expert_activation")
        s_dn = sem("expert_down_product")
        s_acc = sem("expert_added")
        s_lut = sem("lut_chain")
        s_wr = [sem(f"head_weights_loaded{i}") for i in range(2)]
        s_wqh = sem("head_qkv_weights_high")
        s_woh = sem("head_out_weights_high")
        s_wq = sem("head_qkv_weights_split")
        s_wo = sem("head_out_weights_split")
        s_q = sem("q_product")
        s_k = sem("k_product")
        s_v = sem("v_product")
        s_qh = sem("q_high")
        s_ql = sem("q_split")
        s_kh = sem("k_high")
        s_kl = sem("k_split")
        s_vh = sem("v_high")
        s_vl = sem("v_split")
        s_s = sem("scores_bank")
        s_mx = sem("score_max_bank")
        s_e = sem("exps")
        s_t = sem("probs_transposed_bank")
        s_ph = sem("probs_high_bank")
        s_pl = sem("probs_split_bank")
        s_z = sem("z_product")
        s_zh = sem("z_high")
        s_zl = sem("z_split")
        s_o = sem("out_product_bank")
        s_ob = sem("out_product_added")
        s_ri = sem("row_sum_inverted")
        s_fwh = sem("ffn_weights_high")
        s_fw = sem("ffn_weights_split")
        s_fg = sem("ffn_gate_product")
        s_fu = sem("ffn_up_product")
        s_fs = sem("ffn_silu")
        s_fm = sem("ffn_activation")
        s_fh = sem("ffn_activation_high")
        s_fa = sem("ffn_activation_split")
        s_fd = sem("ffn_down_product")

        CONST_DMAS = 12
        block = ctx.enter_context(nc.Block())

        def rows(ap):
            return ap.rearrange("(n p) d -> p n d", p=P)

        SCORE_BANKS = ((0, 2), (1,), (3,))
        PROB_TILES = ((0,), (1, 3), (2,))
        PROB_COLS = (4 * P, 4 * P, 2 * P)

        def score(i):
            if i == 0:
                return bank[2][:, 3 * P:4 * P]
            return bank[{2: 2, 1: 3, 3: 4}[i]][:, 0:(i + 1) * P]

        def prob_at(j):
            return ((0, 0), (1, 0), (2, 0), (1, 3 * P))[j]

        @block.sync
        def _(sp):
            for dst, src in ((w0s, w0), (wabs, wab), (cws, cw), (invfs, invf), (rmsws, rmsw), (wo0s, wo0),
                             (cents, cent), (gbiass, gbias), (iotas, iota16), (lutks, lutk), (luts, lut),
                             (fidxs, fidx)):
                sp.dma_start(dst[:], src).then_inc(s_const, 16)

            with sp.Fori(0, NB) as b:
                sp.wait_ge(s_x0free, b + START)
                sp.dma_start(xin[:], rows(x_in[bass.ds(b, 1), :, :].rearrange("a t d -> (a t) d"))).then_inc(s_x0, 16)
                sp.wait_ge(s_up, b * NE + START)
                for p in range(2):
                    sp.dma_start(wgu[p][:], wexp[p][:, 0:2 * D]).then_inc(s_w[p], 16)
                sp.wait_ge(s_dn, b * NE + START)
                for p in range(2):
                    sp.dma_start(wdn[p][:], wexp[p][:, 2 * D:]).then_inc(s_wd[p], 16)
                with sp.Fori(1, NE // 2) as i:
                    for p in range(2):
                        w = wexp[bass.ds(2 * i + p, 1), :, :].rearrange("a p n -> (a p) n")
                        sp.wait_ge(s_up, b * NE + 2 * i + p - 1 + START)
                        sp.dma_start(wgu[p][:], w[:, 0:2 * D]).then_inc(s_w[p], 16)
                        sp.wait_ge(s_dn, b * NE + 2 * i + p - 1 + START)
                        sp.dma_start(wdn[p][:], w[:, 2 * D:]).then_inc(s_wd[p], 16)
            sp.wait_ge(s_st1, 16 * NB)
            with sp.Fori(0, NB) as b:
                sp.wait_ge(s_x1free, b + START)
                sp.dma_start(xin[:], rows(x1[bass.ds(b, 1), :, :].rearrange("a t d -> (a t) d"))).then_inc(s_x1, 16)
                with sp.Fori(0, NH // 2) as i:
                    for p in range(2):
                        sp.wait_ge(s_wo, b * NH + 2 * i + p - 1 + 2 * START)
                        sp.dma_start(wraw[p][:], wqkvo[bass.ds(2 * i + p, 1), :, :].rearrange("a p n -> (a p) n")
                                     ).then_inc(s_wr[p], 16)

        @block.gpsimd
        def _(pool):
            for s in (s_kept1,):
                pool.sem_inc(s, START)
            pool.memset(ident[:], 0.0).then_inc(s_made, 1)
            pool.memset(ident_bf[:], 0.0).then_inc(s_made, 1)
            pool.memset(causal[:], 0.0).then_inc(s_made, 1)
            pool.memset(half_pi[:], math.pi / 2).then_inc(s_made, 1)
            pool.memset(headsum[:], 1.0).then_inc(s_made, 1)
            pool.wait_ge(s_made, 5)
            for m in (ident, ident_bf):
                pool.affine_select(out=m[:], in_=m[:], compare_op=ALU.not_equal, fill=1.0, base=0,
                                   pattern=[[-1, P]], channel_multiplier=1).then_inc(s_made2, 1)
            pool.affine_select(out=causal[:], in_=causal[:], compare_op=ALU.is_ge, fill=NEG, base=0,
                               pattern=[[-1, P]], channel_multiplier=1).then_inc(s_made2, 1)
            pool.affine_select(out=headsum[:], in_=headsum[:], compare_op=ALU.is_ge, fill=0.0, base=0,
                               pattern=[[-PAIRS, 3]], channel_multiplier=1).then_inc(s_made2, 1)
            pool.wait_ge(s_made2, 4)
            pool.affine_select(out=headsum[:], in_=headsum[:], compare_op=ALU.is_ge, fill=0.0, base=PAIRS - 1,
                               pattern=[[PAIRS, 3]], channel_multiplier=-1).then_inc(s_made2, 1)
            with pool.Fori(0, NB) as b:
                pool.wait_ge(s_acc, (b + 1) * NE + START)
                pool.dma_start(rows(x1[bass.ds(b, 1), :, :].rearrange("a t d -> (a t) d")), xr[:]).then_inc(s_st1, 16)
                pool.wait_ge(s_st1, b * 16 + 16)
                pool.sem_inc(s_kept1, 1)
            pool.sem_inc(s_wo, 2 * START)
            pool.wait_ge(s_lut, 2 * NB * NE + START)
            with pool.Fori(0, NB) as b:
                def low_qkv(g, p):
                    high, low = (w[:].rearrange("p c k n -> p (c k n)") for w in wqkv2[p])
                    pool.wait_ge(s_wqh, g + 1)
                    pool.tensor_tensor(low, wraw[p][:, 0:3 * D], high.bitcast(F32), ALU.subtract).then_inc(s_wq, 1)

                def low_o(g, p):
                    pool.wait_ge(s_woh, g + 1)
                    pool.tensor_tensor(wo2[p][1][:], wraw[p][:, 3 * D:4 * D], wo2[p][0][:].bitcast(F32), ALU.subtract
                                       ).then_inc(s_wo, 1)

                low_qkv(b * NH, 0)
                low_qkv(b * NH + 1, 1)
                low_o(b * NH, 0)
                with pool.Fori(0, NH // 2 - 1) as i:
                    for p in range(2):
                        g = b * NH + 2 * i + p
                        low_o(g + 1, 1 - p)
                        low_qkv(g + 2, p)
                low_o(b * NH + NH - 1, 1)

        @block.scalar
        def _(sc):
            sc.sem_inc(s_st2, 16)
            sc.wait_ge(s_made2, 5)

            def layer_norm_copy(n, b):
                sc.wait_ge(s_hTp[n], b + 1)
                sc.activation(hT[:, 0, :], bank[0][:], ACT.Copy).then_inc(s_hTa[n], 1)

            with sc.Fori(0, NB) as b:
                layer_norm_copy(0, b)
                for hf in range(2):
                    for j, dst in enumerate((al, be, ge, go)):
                        sc.wait_ge(s_pa, b * 8 + hf * 4 + j + 1)
                        if j < 2:
                            sc.activation(dst[:, hf, :], bank[4 + j][0:HALF, :], ACT.Tanh, scale=0.5).then_inc(s_ga, 1)
                        else:
                            sc.activation(dst[:, hf, :], bank[4 + j][0:HALF, :], ACT.Silu).then_inc(s_ga, 1)
                    for j, dst in enumerate((al, be)):
                        sc.wait_ge(s_ga, b * 8 + hf * 4 + j + 1)
                        sc.activation(dst[:, hf, :], dst[:, hf, :], ACT.Copy, scale=0.5, bias=0.5
                                      ).then_inc(s_ab, 1)
                    sc.wait_ge(s_rng, b * 2 + hf + 1)
                    sc.activation(ab[:, hf, :], ang[:, hf, :], ACT.Abs).then_inc(s_abs, 1)
                    sc.activation(sn[:, hf, :], ang[:, hf, :], ACT.Sin)
                    sc.wait_ge(s_abs, b * 2 + hf + 1)
                    sc.activation(cs[:, hf, :], ab[:, hf, :], ACT.Sin, scale=-1.0, bias=half_pi[0:HALF, :]
                                  ).then_inc(s_trig, 1)
                for hf in range(2):
                    sc.wait_ge(s_scan, b * 2 + hf + 1)
                    sc.activation(sn[:, hf, :], oe[:, hf, :], ACT.Square)
                    sc.activation(cs[:, hf, :], oo[:, hf, :], ACT.Square).then_inc(s_sq, 1)
                layer_norm_copy(1, b)
                sc.wait_ge(s_lgc, b + 1)
                sc.activation(aff[:], bia[:], ACT.Exp, scale=-1.0).then_inc(s_ex, 1)

                for e in (0, 1):
                    sc.wait_ge(s_gu, b * NE + e + 1)
                    sc.activation(sg[e][:], bank[e][:], ACT.Silu).then_inc(s_silu, 1)
                with sc.Fori(2, NE, 2) as e:
                    for p in range(2):
                        sc.wait_ge(s_gu, b * NE + e + (p + 1))
                        sc.wait_ge(s_act, b * NE + e + (p - 1))
                        sc.activation(sg[p][:], bank[p][:], ACT.Silu).then_inc(s_silu, 1)

            def high(dst, src, done, scale=1.0):
                sc.activation(dst, src, ACT.Copy, scale=scale).then_inc(done, 1)

            def layer_norm_high(n, b):
                sc.wait_ge(s_hTp[n], b + 1)
                for k in range(KD):
                    high(h2[0][:, k, :], bank[k][:], s_hTa[n])

            sc.wait_ge(s_lut, 2 * NB * NE + START)
            high(fw2[0][:], fws[:], s_fwh)
            with sc.Fori(0, NB) as b:
                def high_qk(g):
                    sc.wait_ge(s_q, g + 1)
                    high(q2[0][:], bank[0][:], s_qh, SCALE)
                    sc.wait_ge(s_k, g + 1)
                    high(k2[0][:], bank[1][:], s_kh)

                def high_v(g, p):
                    sc.wait_ge(s_v, g + 1 + 2 * START)
                    high(v2[p][0][:].rearrange("p t n -> p (t n)"), bank[5][:], s_vh)

                def high_wqkv(g, p, nload):
                    sc.wait_ge(s_wr[p], nload * 16)
                    sc.wait_ge(s_v, g - 1 + 2 * START)
                    high(wqkv2[p][0][:].rearrange("p c k n -> p (c k n)"), wraw[p][:, 0:3 * D], s_wqh)

                def high_wo(g, p):
                    sc.wait_ge(s_o, 2 * g - 2 + 3 * START)
                    high(wo2[p][0][:], wraw[p][:, 3 * D:4 * D], s_woh)

                def softmax(g):
                    for n, tiles in enumerate(SCORE_BANKS):
                        sc.wait_ge(s_mx, 3 * g + n + 1)
                        for i in tiles:
                            ins = sc.activation(pr[:, i, 0:(i + 1) * P], score(i), ACT.Exp, bias=negmax[:, i:i + 1],
                                                accum_out=rsum[:, i:i + 1])
                    ins.then_inc(s_e, 1)

                def high_probs(g):
                    for n in range(3):
                        sc.wait_ge(s_t, 3 * g + n + 1)
                        high(p2[0][:, n, 0:PROB_COLS[n]], bank[2 + n][:, 0:PROB_COLS[n]], s_ph)

                def high_z(g):
                    sc.wait_ge(s_z, g + 1)
                    high(z2[0][:], bank[0][:], s_zh)

                high_wqkv(b * NH, 0, b * (NH // 2) + 1)
                high_wqkv(b * NH + 1, 1, b * (NH // 2) + 1)
                high_wo(b * NH, 0)
                layer_norm_high(2, b)
                high_qk(b * NH)
                high_v(b * NH, 0)
                with sc.Fori(0, NH // 2 - 1) as i:
                    for p in range(2):
                        g = b * NH + 2 * i + p
                        softmax(g)
                        high_qk(g + 1)
                        high_wo(g + 1, 1 - p)
                        high_probs(g)
                        high_v(g + 1, 1 - p)
                        high_wqkv(g + 2, p, b * (NH // 2) + i + 2)
                        high_z(g)
                g = b * NH + NH - 2
                softmax(g)
                high_qk(g + 1)
                high_wo(g + 1, 1)
                high_probs(g)
                high_v(g + 1, 1)
                high_z(g)
                softmax(g + 1)
                high_probs(g + 1)
                high_z(g + 1)
                layer_norm_high(3, b)

                def silu(m):
                    sc.wait_ge(s_fg, b * NM + m + 1)
                    if m >= 2:
                        sc.wait_ge(s_fm, b * NM + m - 1)
                    sc.activation(fsg[m % 2][:], bank[m % 2][:], ACT.Silu).then_inc(s_fs, 1)

                silu(0)
                for m in range(NM):
                    if m + 1 < NM:
                        silu(m + 1)
                    sc.wait_ge(s_fm, b * NM + m + 1)
                    high(fa2[0][:, m, :], ft[m % 2][:], s_fh)
                sc.wait_ge(s_xdone[3], b + 1)
                sc.dma_start(rows(out[bass.ds(b, 1), :, :].rearrange("a t d -> (a t) d")), xr[:]).then_inc(s_st2, 16)
            sc.wait_ge(s_st2, 16 * NB + 16)

        @block.vector
        def _(ve_):
            v = ve_
            for s in (s_x0free, s_x1free, s_acc, s_lut, s_ob):
                v.sem_inc(s, START)
            v.wait_ge(s_const, 16 * CONST_DMAS)
            v.memset(mask[:], SHARED_RATIO).then_inc(s_setup, 1)
            v.memset(fws[:], 0.0)
            for k in range(KD):
                for j in range(2):
                    v.tensor_copy(wabr[:, k, j].rearrange("p h (a c) -> p (h a) c", c=PAIRS),
                                  wabs[:, k, j, :].unsqueeze(2).to_broadcast([P, HEADS0, PAIRS]))
            v.tensor_scalar(cws[:, 0], cws[:, 0], invfs[:, 0:1], -1.0, ALU.mult, ALU.mult)
            v.tensor_scalar(cws[:, 1], cws[:, 1], invfs[:, 0:1], None, ALU.mult).then_inc(s_setup, 1)
            v.wait_ge(s_setup, 2)

            def rsqrt(n, link, extra):
                link(v.tensor_scalar(ry[:, 0:n].bitcast(I32), va[:, 0:n].bitcast(I32), -0.5, RSQRT_SEED,
                                     ALU.mult, ALU.add))
                for _ in range(3):
                    link(v.tensor_tensor(rt[:, 0:n], ry[:, 0:n], ry[:, 0:n], ALU.mult))
                    link(v.scalar_tensor_tensor(rt[:, 0:n], rt[:, 0:n], -0.5, va[:, 0:n], ALU.mult, ALU.mult))
                    link(v.scalar_tensor_tensor(ry[:, 0:n], rt[:, 0:n], 1.5, ry[:, 0:n], ALU.add, ALU.mult))

            def layer_norm(n, b, src):
                done = [0]

                def link(ins):
                    done[0] += 1
                    ins.then_inc(s_lnc[n], 1)
                    v.wait_ge(s_lnc[n], b * LN_LINKS + done[0])

                for i in range(NT):
                    ins = v.bn_stats(stats[:, i, :], src[:, i, :])
                link(ins)
                v.tensor_tensor(mv[:, :, 0], stats[:, :, 1], stats[:, :, 4], ALU.add)
                v.tensor_tensor(rt[:, 0:NT], stats[:, :, 1], stats[:, :, 4], ALU.subtract)
                link(v.tensor_tensor(mv[:, :, 1], stats[:, :, 2], stats[:, :, 5], ALU.add))
                v.tensor_scalar(mv[:, :, 0], mv[:, :, 0], 0.5, None, ALU.mult)
                v.tensor_scalar(mv[:, :, 1], mv[:, :, 1], 1.0 / D, EPS, ALU.mult, ALU.add)
                link(v.tensor_tensor(rt[:, 0:NT], rt[:, 0:NT], rt[:, 0:NT], ALU.mult))
                link(v.scalar_tensor_tensor(va[:, 0:NT], rt[:, 0:NT], 0.25, mv[:, :, 1], ALU.mult, ALU.add))
                rsqrt(NT, link, 0)
                assert done[0] == LN_LINKS
                for i in range(NT):
                    ins = v.tensor_scalar(xn[:, i, :], src[:, i, :], mv[:, i, 0:1], ry[:, i:i + 1],
                                          ALU.subtract, ALU.mult)
                ins.then_inc(s_xn[n], 1)
                if n < 2:
                    v.wait_ge(s_hTp[n], b + 1)
                    v.tensor_copy(hT[:, 1, :], bank[1][:]).then_inc(s_hTv[n], 1)
                else:
                    for k in range(KD):
                        v.wait_ge(s_hTa[n], b * KD + k + 1)
                        low(h2, bank[k][:], s_hTv[n], lambda part: part[:, k, :])

            def low(parts, src, done, at=lambda part: part[:], scale=None):
                high_ = at(parts[0]).bitcast(F32)
                if scale is None:
                    v.tensor_tensor(at(parts[1]), src, high_, ALU.subtract).then_inc(done, 1)
                else:
                    v.scalar_tensor_tensor(at(parts[1]), src, scale, high_, ALU.mult, ALU.subtract).then_inc(done, 1)

            with v.Fori(0, NB) as b:
                v.wait_ge(s_x0, (b + 1) * 16)
                layer_norm(0, b, xin)
                done = [0]

                def link(ins):
                    done[0] += 1
                    ins.then_inc(s_l0, 1)
                    v.wait_ge(s_l0, b * L0_LINKS + done[0])

                def conv_tile(n, dst, hf, quant, first):
                    v.wait_ge(s_pv, b * 8 + n + 1)
                    src = bank[n % 4][0:HALF, :]
                    tap = [cws[:, quant, hf, j:j + 1] for j in range(TAPS)]
                    d = dst[:, hf, :]
                    if first:
                        link(v.tensor_scalar(d, src, tap[TAPS - 1], None, ALU.mult))
                    else:
                        link(v.scalar_tensor_tensor(d, src, tap[TAPS - 1], d, ALU.mult, ALU.add))
                    for s in range(1, TAPS):
                        ins = v.scalar_tensor_tensor(d[:, s:T], src[:, 0:T - s], tap[TAPS - 1 - s], d[:, s:T],
                                                     ALU.mult, ALU.add)
                        if s < TAPS - 1:
                            link(ins)
                    ins.then_inc(s_cv, 1)
                    v.wait_ge(s_cv, b * 8 + n + 1)

                for hf in range(2):
                    conv_tile(4 * hf + 0, ang, hf, 0, True)
                    conv_tile(4 * hf + 1, ang, hf, 1, False)
                    a, n_ = ang[:, hf, :], turns[:, hf, :]
                    link(v.tensor_scalar(n_, a, 1.0 / TWO_PI, ROUND, ALU.mult, ALU.add))
                    link(v.tensor_scalar(n_, n_, ROUND, None, ALU.subtract))
                    link(v.scalar_tensor_tensor(a, n_, -PI_HI, a, ALU.mult, ALU.add))
                    link(v.scalar_tensor_tensor(a, n_, -PI_LO, a, ALU.mult, ALU.add))
                    v.tensor_scalar(a, a, PI_MAX, -PI_MAX, ALU.min, ALU.max).then_inc(s_rng, 1)
                    conv_tile(4 * hf + 2, ve, hf, 2, True)
                    conv_tile(4 * hf + 3, vo, hf, 3, True)
                for hf in range(2):
                    v.wait_ge(s_trig, b * 2 + hf + 1)
                    v.wait_ge(s_ab, b * 4 + 2 * hf + 2)
                    h = (slice(None), hf, slice(None))
                    v.tensor_tensor(cs[h], cs[h], be[h], ALU.mult)
                    link(v.tensor_tensor(sn[h], sn[h], be[h], ALU.mult))
                    v.tensor_tensor(t1[h], ve[h], cs[h], ALU.mult)
                    v.tensor_tensor(t2[h], vo[h], sn[h], ALU.mult)
                    v.tensor_tensor(t3[h], vo[h], cs[h], ALU.mult)
                    link(v.tensor_tensor(t4[h], ve[h], sn[h], ALU.mult))
                    v.tensor_tensor(t1[h], t1[h], t2[h], ALU.subtract)
                    link(v.tensor_tensor(t3[h], t3[h], t4[h], ALU.add))
                    v.tensor_tensor_scan(oe[h], al[h], t1[h], 0.0, ALU.mult, ALU.add)
                    v.tensor_tensor_scan(oo[h], al[h], t3[h], 0.0, ALU.mult, ALU.add).then_inc(s_scan, 1)
                v.wait_ge(s_scan, b * 2 + 2)
                v.wait_ge(s_ga, b * 8 + 8)
                for hf in range(2):
                    h = (slice(None), hf, slice(None))
                    v.scalar_tensor_tensor(ge[h], ge[h], rmsws[:, 0:1], oe[h], ALU.mult, ALU.mult)
                    ins = v.scalar_tensor_tensor(go[h], go[h], rmsws[:, 1:2], oo[h], ALU.mult, ALU.mult)
                link(ins)
                v.wait_ge(s_ms, b + 1)
                link(v.tensor_scalar(va[:], bank[2][:, 0:NT * HEADS0], 1.0 / (2 * PAIRS), EPS, ALU.mult, ALU.add))
                rsqrt(NT * HEADS0, link, 0)
                v.tensor_copy(rexp[:].rearrange("p t h c -> p (t h) c"),
                              ry[:].unsqueeze(2).to_broadcast([P, NT * HEADS0, PAIRS])).then_inc(s_re, 1)
                v.wait_ge(s_rT, b + 1)
                for hf in range(2):
                    h = (slice(None), hf, slice(None))
                    v.tensor_tensor(ge[h], ge[h], bank[4 + hf][0:HALF, :], ALU.mult)
                    ins = v.tensor_tensor(go[h], go[h], bank[4 + hf][0:HALF, :], ALU.mult)
                ins.then_inc(s_y, 1)
                assert done[0] == L0_LINKS, done[0]
                v.wait_ge(s_o0, b + 1)
                v.wait_ge(s_kept1, b + START)
                for i in range(2):
                    ins = v.tensor_tensor(xr[:, 2 * i:2 * i + 2, :].rearrange("p n d -> p (n d)"), bank[6 + i][:],
                                          xin[:, 2 * i:2 * i + 2, :].rearrange("p n d -> p (n d)"), ALU.add)
                ins.then_inc(s_x0free, 1)
                v.wait_ge(s_x0free, b + 1 + START)

                layer_norm(1, b, xr)
                rdone = [0]

                def rlink(ins):
                    rdone[0] += 1
                    ins.then_inc(s_rc, 1)
                    v.wait_ge(s_rc, b * RC_LINKS + rdone[0])

                v.wait_ge(s_lg, b + 1)
                v.tensor_scalar(bia[:], bank[2][:, 0:NT * NEXP].rearrange("p (t e) -> p t e", t=NT), -87.0, None,
                                ALU.max).then_inc(s_lgc, 1)
                v.wait_ge(s_ex, b + 1)
                rlink(v.tensor_scalar(r1[:], aff[:], 1.0, None, ALU.add))
                rlink(v.reciprocal(aff[:], r1[:]))
                rlink(v.tensor_tensor(bia[:], aff[:], gbiass[:], ALU.add))
                for turn in range(2):
                    rlink(v.tensor_reduce(m1[:], bia[:], AX_X, ALU.max))
                    rlink(v.tensor_tensor(r1[:], bia[:], m1[:].unsqueeze(2).to_broadcast([P, NT, NEXP]), ALU.is_lt))
                    rlink(v.scalar_tensor_tensor(r1[:].rearrange("p t e -> p (t e)"),
                                                 r1[:].rearrange("p t e -> p (t e)"), float(NE),
                                                 iotas[:].rearrange("p t e -> p (t e)"), ALU.mult, ALU.add))
                    rlink(v.tensor_reduce(m1[:], r1[:], AX_X, ALU.min))
                    dst = pick if turn == 0 else r2
                    rlink(v.tensor_tensor(dst[:], iotas[:], m1[:].unsqueeze(2).to_broadcast([P, NT, NEXP]),
                                          ALU.is_equal))
                    if turn == 0:
                        rlink(v.scalar_tensor_tensor(bia[:].rearrange("p t e -> p (t e)"),
                                                     pick[:].rearrange("p t e -> p (t e)"), -3.0e38,
                                                     bia[:].rearrange("p t e -> p (t e)"), ALU.mult, ALU.add))
                rlink(v.tensor_tensor(pick[:], pick[:], r2[:], ALU.add))
                rlink(v.tensor_tensor(pick[:], pick[:], aff[:], ALU.mult))
                rlink(v.tensor_reduce(m1[:], pick[:], AX_X, ALU.add))
                rlink(v.tensor_scalar(m1[:], m1[:], 1e-9, None, ALU.add))
                rlink(v.reciprocal(m1[:], m1[:]))
                assert rdone[0] == RC_LINKS, rdone[0]
                v.tensor_tensor(mask[:, :, 0:NEXP], pick[:], m1[:].unsqueeze(2).to_broadcast([P, NT, NEXP]),
                                ALU.mult).then_inc(s_mask, 1)
                v.wait_ge(s_mask, b + 1)

                def activate(g, p):
                    v.wait_ge(s_silu, g + 1)
                    v.wait_ge(s_up, g + 1 + START)
                    v.tensor_tensor(act[p][:], sg[p][:], bank[2 + p][:], ALU.mult).then_inc(s_act, 1)

                def accumulate(g, e, p):
                    v.wait_ge(s_dn, g + 1 + START)
                    v.wait_ge(s_acc, g + START)
                    for i in range(NT):
                        ins = v.scalar_tensor_tensor(xr[:, i, :], bank[4 + 2 * p + i // 2][:, (i % 2) * D:(i % 2 + 1) * D],
                                                     mask[:, i, bass.ds(e, 1)], xr[:, i, :], ALU.mult, ALU.add)
                    ins.then_inc(s_acc, 1)

                def lut_step(g, e):
                    v.tensor_scalar(ftmp[:], fidxs[:, bass.ds(b * LC, LC)], lutks[:, bass.ds(e, 1)],
                                    luts[:, bass.ds(e, 1)], ALU.is_equal, ALU.mult).then_inc(s_lut, 1)
                    v.wait_ge(s_lut, 2 * g + 1 + START)
                    v.tensor_tensor(fws[:, bass.ds(b * LC, LC)], fws[:, bass.ds(b * LC, LC)], ftmp[:],
                                    ALU.add).then_inc(s_lut, 1)

                activate(b * NE, 0)
                with v.Fori(0, NE - 2, 2) as e:
                    for p in range(2):
                        g = b * NE + e + p
                        v.wait_ge(s_lut, 2 * g + START)
                        lut_step(g, e + p)
                        activate(g + 1, 1 - p)
                        accumulate(g, e + p, p)
                activate(b * NE + NE - 1, 1)
                accumulate(b * NE + NE - 2, NE - 2, 0)
                accumulate(b * NE + NE - 1, NE - 1, 1)
                for e in (NE - 2, NE - 1):
                    v.wait_ge(s_lut, 2 * (b * NE + e) + START)
                    lut_step(b * NE + e, e)

            v.wait_ge(s_lut, 2 * NB * NE + START)
            v.wait_ge(s_fwh, 1)
            low(fw2, fws[:], s_fw)
            with v.Fori(0, NB) as b:
                v.wait_ge(s_x1, (b + 1) * 16)
                layer_norm(2, b, xin)
                v.wait_ge(s_st2, b * 16 + 16)
                v.tensor_copy(xr[:], xin[:]).then_inc(s_x1free, 1)
                v.wait_ge(s_x1free, b + 1 + START)

                def low_qk(g):
                    v.wait_ge(s_qh, g + 1)
                    low(q2, bank[0][:], s_ql, scale=SCALE)
                    v.wait_ge(s_kh, g + 1)
                    low(k2, bank[1][:], s_kl)

                def low_v(g, p):
                    v.wait_ge(s_vh, g + 1)
                    low(v2[p], bank[5][:], s_vl, lambda part: part[:].rearrange("p t n -> p (t n)"))

                def score_max(g):
                    for n, tiles in enumerate(SCORE_BANKS):
                        v.wait_ge(s_s, 3 * g + n + 1)
                        for i in tiles:
                            ins = v.tensor_reduce(negmax[:, i:i + 1], score(i), AX_X, ALU.max, negate=True)
                        ins.then_inc(s_mx, 1)

                def low_probs(g):
                    for n in range(3):
                        v.wait_ge(s_ph, 3 * g + n + 1)
                        low(p2, bank[2 + n][:, 0:PROB_COLS[n]], s_pl, lambda part: part[:, n, 0:PROB_COLS[n]])

                def low_z(g):
                    v.wait_ge(s_zh, g + 1)
                    low(z2, bank[0][:], s_zl)

                def invert_sums(g):
                    v.wait_ge(s_ob, g + START)
                    v.reciprocal(rinv[:], rsum[:]).then_inc(s_ri, 1)

                def add_out(g):
                    v.wait_ge(s_ri, g + 1)
                    v.wait_ge(s_ob, g + START)
                    for n in range(2):
                        v.wait_ge(s_o, 2 * g + n + 1 + 3 * START)
                        for i in (2 * n, 2 * n + 1):
                            ins = v.scalar_tensor_tensor(xr[:, i, :], bank[6 + n][:, (i % 2) * D:(i % 2 + 1) * D],
                                                         rinv[:, i:i + 1], xr[:, i, :], ALU.mult, ALU.add)
                    ins.then_inc(s_ob, 1)

                def head(h, p, first=False, last=False):
                    g = b * NH + h
                    score_max(g)
                    if not first:
                        add_out(g - 1)
                    if not last:
                        low_qk(g + 1)
                    low_probs(g)
                    invert_sums(g)
                    if not last:
                        low_v(g + 1, 1 - p)
                    low_z(g)

                low_qk(b * NH)
                low_v(b * NH, 0)
                head(0, 0, first=True)
                with v.Fori(0, NH // 2 - 1) as i:
                    for p in (1, 0):
                        head(2 * i + (2 - p), p)
                head(NH - 1, 1, last=True)
                add_out(b * NH + NH - 1)
                v.wait_ge(s_ob, b * NH + NH + START)
                layer_norm(3, b, xr)

                def ffn_product(m):
                    v.wait_ge(s_fs, b * NM + m + 1)
                    v.wait_ge(s_fu, b * NM + m + 1)
                    if m >= 2:
                        v.wait_ge(s_fa, b * NM + m - 1)
                    v.tensor_tensor(ft[m % 2][:], fsg[m % 2][:], bank[2 + m % 2][:], ALU.mult).then_inc(s_fm, 1)

                def ffn_low(m):
                    v.wait_ge(s_fh, b * NM + m + 1)
                    low(fa2, ft[m % 2][:], s_fa, lambda part: part[:, m, :])

                ffn_product(0)
                for m in range(NM):
                    if m + 1 < NM:
                        ffn_product(m + 1)
                    ffn_low(m)
                v.wait_ge(s_fd, b + 1)
                for i in range(2):
                    x2 = xr[:, 2 * i:2 * i + 2, :].rearrange("p n d -> p (n d)")
                    ins = v.tensor_tensor(x2, bank[4 + i][:], x2, ALU.add)
                ins.then_inc(s_xdone[3], 1)

        @block.tensor
        def _(pe):
            mm = pe.matmul
            for s, n in ((s_dn, 1), (s_up, 1), (s_o, 3), (s_v, 2)):
                pe.sem_inc(s, n * START)
            pe.wait_ge(s_const, 16 * CONST_DMAS)
            pe.wait_ge(s_made2, 5)
            pe.wait_ge(s_setup, 2)

            def layer_norm_transpose(n, b):
                pe.wait_ge(s_xn[n], b + 1)
                for k in range(KD):
                    for i in range(NT):
                        ins = pe.transpose(bank[k][:, i * P:(i + 1) * P], xn[:, i, k * P:(k + 1) * P], ident[:])
                ins.then_inc(s_hTp[n], 1)
                pe.wait_ge(s_hTa[n], (b + 1) * (1 if n < 2 else KD))
                pe.wait_ge(s_hTv[n], (b + 1) * (1 if n < 2 else KD))

            def project(dst, w):
                for k in range(KD):
                    ins = mm(dst, w(k), hT[:, k, :], start=(k == 0), stop=(k == KD - 1))
                return ins

            with pe.Fori(0, NB) as b:
                layer_norm_transpose(0, b)
                for hf in range(2):
                    def w_of(q):
                        return lambda k: w0s[:, k, q, hf, :]

                    def ab_of(j):
                        return lambda k: wabr[:, k, j, hf, :]

                    plan = [("v", 0, w_of(0)), ("v", 1, w_of(1)), ("a", 0, ab_of(0)), ("a", 1, ab_of(1)),
                            ("v", 2, w_of(2)), ("v", 3, w_of(3)), ("a", 2, w_of(4)), ("a", 3, w_of(5))]
                    for kind, j, w in plan:
                        if hf == 1:
                            pe.wait_ge(s_cv if kind == "v" else s_ga, b * 8 + j + 1)
                        dst = bank[j if kind == "v" else 4 + j][0:HALF, :]
                        project(dst, w).then_inc(s_pv if kind == "v" else s_pa, 1)
                pe.wait_ge(s_cv, b * 8 + 8)
                for hf in range(2):
                    pe.wait_ge(s_sq, b * 2 + hf + 1)
                    for i in range(NT):
                        dst = bank[2][:, i * HEADS0 + 3 * hf:i * HEADS0 + 3 * hf + 3]
                        mm(dst, sn[:, hf, i * P:(i + 1) * P], headsum[:], start=True, stop=False)
                        ins = mm(dst, cs[:, hf, i * P:(i + 1) * P], headsum[:], start=False, stop=True)
                ins.then_inc(s_ms, 1)
                pe.wait_ge(s_re, b + 1)
                pe.wait_ge(s_ga, b * 8 + 8)
                for hf in range(2):
                    for i in range(NT):
                        ins = pe.transpose(bank[4 + hf][0:HALF, i * P:(i + 1) * P],
                                           rexp[:, i, 3 * hf:3 * hf + 3, :].rearrange("p h c -> p (h c)"), ident[:])
                ins.then_inc(s_rT, 1)
                pe.wait_ge(s_y, b + 1)
                for i in range(NT):
                    dst = bank[6 + i // 2][:, (i % 2) * D:(i % 2 + 1) * D]
                    n = 0
                    for hf in range(2):
                        for par, src in enumerate((ge, go)):
                            ins = mm(dst, src[:, hf, i * P:(i + 1) * P], wo0s[:, hf, par, :], start=(n == 0),
                                     stop=(n == 3))
                            n += 1
                ins.then_inc(s_o0, 1)

                layer_norm_transpose(1, b)
                for i in range(NT):
                    for k in range(KD):
                        ins = mm(bank[2][:, i * NEXP:(i + 1) * NEXP], hT[:, k, i * P:(i + 1) * P], cents[:, k, :],
                                 start=(k == 0), stop=(k == KD - 1))
                ins.then_inc(s_lg, 1)

                def gate_up(g, p, nload):
                    pe.wait_ge(s_w[p], nload * 16)
                    pe.wait_ge(s_silu, g - 1)
                    project(bank[p][:], lambda k: wgu[p][:, k * P:(k + 1) * P]).then_inc(s_gu, 1)
                    pe.wait_ge(s_act, g - 1)
                    project(bank[2 + p][:], lambda k: wgu[p][:, D + k * P:D + (k + 1) * P]).then_inc(s_up, 1)

                def gate_up_first(g, p, nload):
                    pe.wait_ge(s_w[p], nload * 16)
                    pe.wait_ge(s_lgc, b + 1)
                    project(bank[p][:], lambda k: wgu[p][:, k * P:(k + 1) * P]).then_inc(s_gu, 1)
                    project(bank[2 + p][:], lambda k: wgu[p][:, D + k * P:D + (k + 1) * P]).then_inc(s_up, 1)

                def down(g, p, nload):
                    pe.wait_ge(s_wd[p], nload * 16)
                    pe.wait_ge(s_act, g + 1)
                    for i in range(NT):
                        ins = mm(bank[4 + 2 * p + i // 2][:, (i % 2) * D:(i % 2 + 1) * D],
                                 act[p][:, i * P:(i + 1) * P], wdn[p][:], start=True, stop=True)
                    ins.then_inc(s_dn, 1)

                gate_up_first(b * NE, 0, b * (NE // 2) + 1)
                gate_up_first(b * NE + 1, 1, b * (NE // 2) + 1)
                down(b * NE, 0, b * (NE // 2) + 1)
                with pe.Fori(0, NE // 2 - 1) as i:
                    for p in (1, 0):
                        g = b * NE + 2 * i + (2 - p)
                        gate_up(g + 1, 1 - p, b * (NE // 2) + i + 2)
                        pe.wait_ge(s_acc, g - 1 + START)
                        down(g, p, b * (NE // 2) + i + (1 if p else 2))
                pe.wait_ge(s_acc, b * NE + NE - 2 + START)
                down(b * NE + NE - 1, 1, b * (NE // 2) + NE // 2)

            def mm3(dst, w, x, start, stop):
                mm(dst, w[0], x[0], start=start, stop=False)
                mm(dst, w[0], x[1], start=False, stop=False)
                return mm(dst, w[1], x[0], start=False, stop=stop)

            def parts(pair, at):
                return [at(t) for t in pair]

            def project3(dst, w_at):
                for k in range(KD):
                    ins = mm3(dst, [w_at(part, k) for part in range(2)], parts(h2, lambda t: t[:, k, :]),
                              k == 0, k == KD - 1)
                return ins

            with pe.Fori(0, NB) as b:
                layer_norm_transpose(2, b)

                def make_qk(g, p):
                    pe.wait_ge(s_wq, g + 1)
                    project3(bank[0][:], lambda part, k: wqkv2[p][part][:, 0, k, :]).then_inc(s_q, 1)
                    project3(bank[1][:], lambda part, k: wqkv2[p][part][:, 1, k, :]).then_inc(s_k, 1)

                def make_v(g, p):
                    for i in range(NT):
                        for k in range(KD):
                            ins = mm3(bank[5][:, i * P:(i + 1) * P], parts(h2, lambda t: t[:, k, i * P:(i + 1) * P]),
                                      parts(wqkv2[p], lambda t: t[:, 2, k, :]), k == 0, k == KD - 1)
                    ins.then_inc(s_v, 1)

                def scores(g):
                    pe.wait_ge(s_ql, g + 1)
                    pe.wait_ge(s_kl, g + 1)
                    for tiles in SCORE_BANKS:
                        for i in tiles:
                            dst = score(i)
                            mm3(dst, parts(q2, lambda t: t[:, i * P:(i + 1) * P]),
                                parts(k2, lambda t: t[:, 0:(i + 1) * P]), True, False)
                            ins = mm(dst[:, i * P:(i + 1) * P], ident_bf[:], causal[:], start=False, stop=True)
                        ins.then_inc(s_s, 1)

                def transpose_probs(g):
                    pe.wait_ge(s_e, g + 1)
                    for tiles in PROB_TILES:
                        for j in tiles:
                            n, c = prob_at(j)
                            for i in range(j, NT):
                                at = c + (i - j) * P
                                ins = pe.transpose(bank[2 + n][:, at:at + P], pr[:, i, j * P:(j + 1) * P], ident[:])
                        ins.then_inc(s_t, 1)

                def make_z(g, p):
                    done = 0
                    for n, tiles in enumerate(PROB_TILES):
                        pe.wait_ge(s_pl, 3 * g + n + 1)
                        for j in tiles:
                            n_, c = prob_at(j)
                            done += 1
                            ins = mm3(bank[0][:, j * P:T], parts(v2[p], lambda t: t[:, j, :]),
                                      parts(p2, lambda t: t[:, n_, c:c + T - j * P]), done == 1, done == NT)
                    ins.then_inc(s_z, 1)

                def project_out(g, p):
                    pe.wait_ge(s_wo, g + 1 + 2 * START)
                    pe.wait_ge(s_zl, g + 1)
                    pe.wait_ge(s_ob, g + START)
                    for n in range(2):
                        for i in (2 * n, 2 * n + 1):
                            ins = mm3(bank[6 + n][:, (i % 2) * D:(i % 2 + 1) * D],
                                      parts(z2, lambda t: t[:, i * P:(i + 1) * P]), parts(wo2[p], lambda t: t[:]),
                                      True, True)
                        ins.then_inc(s_o, 1)

                def head(h, p, first=False, last=False):
                    g = b * NH + h
                    if not first:
                        project_out(g - 1, 1 - p)
                    if not last:
                        make_qk(g + 1, 1 - p)
                    transpose_probs(g)
                    if not last:
                        pe.wait_ge(s_vl, g + 1)
                        make_v(g + 1, 1 - p)
                        pe.wait_ge(s_ql, g + 2)
                    make_z(g, p)
                    if not last:
                        scores(g + 1)

                make_qk(b * NH, 0)
                make_v(b * NH, 0)
                scores(b * NH)
                head(0, 0, first=True)
                with pe.Fori(0, NH // 2 - 1) as i:
                    for p in (1, 0):
                        head(2 * i + (2 - p), p)
                head(NH - 1, 1, last=True)
                project_out(b * NH + NH - 1, 1)

                layer_norm_transpose(3, b)
                pe.wait_ge(s_fw, 1)
                gate, up, down = zip(ffn_weights(0), ffn_weights(1))
                for m in range(NM):
                    m0 = m * P
                    if m >= 2:
                        pe.wait_ge(s_fs, b * NM + m - 1)
                    project3(bank[m % 2][:], lambda part, k: gate[part][:, k, m0:m0 + P]).then_inc(s_fg, 1)
                    if m >= 2:
                        pe.wait_ge(s_fm, b * NM + m - 1)
                    project3(bank[2 + m % 2][:], lambda part, k: up[part][:, k, m0:m0 + P]).then_inc(s_fu, 1)
                pe.wait_ge(s_fa, b * NM + NM)
                for i in range(NT):
                    for m in range(NM):
                        ins = mm3(bank[4 + i // 2][:, (i % 2) * D:(i % 2 + 1) * D],
                                  parts(fa2, lambda t: t[:, m, i * P:(i + 1) * P]), [w[:, m, :] for w in down],
                                  m == 0, m == NM - 1)
                ins.then_inc(s_fd, 1)


_OUT = (NB, T, D)


def kernel(**inputs):
    import concourse.bacc as bacc
    from concourse.bass_utils import run_bass_kernel_spmd

    a = {k: np.asarray(v) for k, v in inputs.items()}

    def halves(w, parity):
        return w[..., parity::2].reshape(*w.shape[:-1], 2, HALF)

    def kt(w):
        return w.reshape(KD, P, -1).transpose(1, 0, 2)

    wq, wk, wv, wg = (a["L0_attn_W" + c] for c in "qkvg")
    w0 = np.stack([halves(wq, 0), halves(wk, 0), halves(wv, 0), halves(wv, 1), halves(wg, 0), halves(wg, 1)], 1)
    w0 = kt(w0.reshape(D, -1)).reshape(P, KD, 6, 2, HALF)
    wab = kt(np.concatenate([a["L0_attn_Wa"], a["L0_attn_Wb"]], 1)).reshape(P, KD, 2, HEADS0)
    cq, ck, cv = (a["L0_attn_conv_" + c].T for c in "qkv")
    cw = np.stack([halves(cq, 0), halves(ck, 0), halves(cv, 0), halves(cv, 1)])
    cw = cw.transpose(3, 0, 2, 1)
    invf = np.tile((1.0 / 10000.0 ** (np.arange(0, 64, 2, dtype=np.float32) / np.float32(64))).astype(np.float32), 3)
    rw = np.tile(a["L0_attn_rms_w"].reshape(PAIRS, 2), (3, 1))
    wo0 = a["L0_attn_Wo"].reshape(2, HALF, 2, D).transpose(1, 0, 2, 3)
    cent = kt(a["L0_ffn_centroids"].T)
    gb = np.tile(a["L0_ffn_gate_bias"], (P, NT, 1))
    gate = np.concatenate([a["L0_ffn_wg"], a["L0_ffn_wg_s"].reshape(D, NSHARED, P).transpose(1, 0, 2)])
    up = np.concatenate([a["L0_ffn_wu"], a["L0_ffn_wu_s"].reshape(D, NSHARED, P).transpose(1, 0, 2)])
    down = np.concatenate([a["L0_ffn_wd"], a["L0_ffn_wd_s"].reshape(NSHARED, P, D)])

    def ekt(w):
        return w.reshape(NE, KD, P, P).transpose(0, 2, 1, 3).reshape(NE, P, D)

    wexp = np.concatenate([ekt(gate), ekt(up), down], 2)
    iota = np.tile(np.arange(NEXP, dtype=np.float32), (P, NT, 1))
    lutk = np.tile(np.arange(NE, dtype=np.float32), (P, 1))
    qkv = np.stack([a["L1_attn_W_Q"], a["L1_attn_W_K"], a["L1_attn_W_V"]], 1)
    qkv = qkv.reshape(NH, 3, DH, KD, P).transpose(0, 4, 1, 3, 2).reshape(NH, P, -1)
    wqkvo = np.concatenate([qkv, a["L1_attn_W_O"].reshape(D, NH, DH).transpose(1, 2, 0)], 2)
    gi, ui, di = (a[f"L1_ffn_{n}_idx"] for n in ("gate", "up", "down"))

    def padded(idx):
        return np.concatenate([idx, np.full((INTER_PAD - INTER, D), LUTN, idx.dtype)])

    fidx = np.concatenate([kt(padded(gi).T).reshape(P, -1), kt(padded(ui).T).reshape(P, -1),
                           padded(di.T).reshape(NM, P, D).transpose(1, 0, 2).reshape(P, -1)], 1)
    lut = np.zeros((P, NE), np.float32)
    lut[:, :LUTN] = a["L1_ffn_lut"]

    named = dict(x=a["L0_attn_hidden_states"], w0=w0, wab=wab, cw=cw, invf=invf[:, None], rmsw=rw, wo0=wo0, cent=cent,
                 gbias=gb, wexp=wexp, iota=iota, lutk=lutk, wqkvo=wqkvo, fidx=fidx, lut=lut)
    nc = bacc.Bacc("TRN2", target_bir_lowering=False, num_devices=1)
    arrays, args = {}, []
    for name, arr in named.items():
        arr = np.ascontiguousarray(arr)
        arrays[f"in_{name}"] = arr
        args.append(nc.dram_tensor(f"in_{name}", arr.shape, mybir.dt.from_np(arr.dtype), kind="ExternalInput").ap())
    args.append(nc.dram_tensor("out_x", _OUT, F32, kind="ExternalOutput").ap())
    two_layer_program(nc, *args)
    r = run_bass_kernel_spmd(nc, [arrays], core_ids=[0])
    return r.results[0]["out_x"]
```

```python
from contextlib import ExitStack
import math

import numpy as np
import concourse.bass as bass
from concourse import mybir

ALU = mybir.AluOpType
ACT = mybir.ActivationFunctionType
F32 = mybir.dt.float32
F32R = mybir.dt.float32r
BF16 = mybir.dt.bfloat16
I32 = mybir.dt.int32
AX_X = mybir.AxisListType.X

P = 128
NB, T, D = 8, 512, 256
NT = T // P
KD = D // P
HEADS0, PAIRS = 6, 32
HALF = HEADS0 * PAIRS // 2
TAPS = 4
EPS = 1e-5
NEXP, NSHARED = 16, 2
NE = NEXP + NSHARED
SHARED_RATIO = 0.1
NH, DH = 16, 128
NPAIR = NH // 2
QUADS = NH // 4 - 1
SCALE = 1.0 / math.sqrt(DH)
NEG = -1e10
INTER = 688
INTER_PAD = -(-INTER // P) * P
NM = INTER_PAD // P
LUTN = 16
FW = KD * INTER_PAD * 2 + NM * D
LC = FW // NB

TWO_PI = 2 * math.pi
ROUND = 1.5 * 2.0 ** 23
PI_HI = 6.28125
PI_LO = TWO_PI - PI_HI
PI_MAX = 3.1415925
RSQRT_SEED = float(0x5F3759DF)
START = 1
LUT_STEPS = 2
LN_LINKS = 14
L0_LINKS = 50
RC_LINKS = 19


def two_layer_program(nc, x_in, w0, wab, cw, invf, rmsw, wo0, cent, gbias, wexp, iota16, lutk, wpair, fidx, lut, out):
    ctx = ExitStack()
    with ctx:
        def sb(name, shape, dt=F32):
            return ctx.enter_context(nc.sbuf_tensor(name, shape, dt))

        def sem(name):
            return ctx.enter_context(nc.semaphore(name))

        x1 = nc.dram_tensor("x1_between_stages", [NB + 1, T, D], F32, kind="Internal").ap()
        bank = [ctx.enter_context(nc.psum_tensor(f"bank{i}", [P, 512], F32)) for i in range(8)]

        ident = sb("ident", [P, P])
        ident_bf = sb("ident_bf", [P, P], BF16)
        causal = sb("causal", [P, P], BF16)
        half_pi = sb("half_pi", [P, 1])
        fws = sb("fws", [P, FW])
        xin = sb("xin", [P, NT, D])
        xr = sb("xr", [P, NT, D])
        xn = sb("xn", [P, NT, D])
        stats = sb("stats", [P, NT, 6])
        mv = sb("mv", [P, NT, 2])
        va = sb("va", [P, NT * HEADS0])
        ry = sb("ry", [P, NT * HEADS0])
        rt = sb("rt", [P, NT * HEADS0])

        stage1 = ExitStack()

        def sb1(name, shape, dt=F32):
            return stage1.enter_context(nc.sbuf_tensor(name, shape, dt))

        hT = sb1("hT", [P, KD, T])
        headsum = sb1("headsum", [HALF, 3])
        w0s = sb1("w0s", [P, KD, 6, 2, HALF])
        wabs = sb1("wabs", [P, KD, 2, HEADS0])
        wabr = sb1("wabr", [P, KD, 2, 2, HALF])
        cws = sb1("cws", [HALF, 4, 2, TAPS])
        invfs = sb1("invfs", [HALF, 1])
        rmsws = sb1("rmsws", [HALF, 2])
        wo0s = sb1("wo0s", [HALF, 2, 2, D])
        cents = sb1("cents", [P, KD, NEXP])
        gbiass = sb1("gbiass", [P, NT, NEXP])
        iotas = sb1("iotas", [P, NT, NEXP])
        lutks = sb1("lutks", [P, NE])
        luts = sb1("luts", [P, NE])
        fidxs = sb1("fidxs", [P, LC], I32)
        ftmp = sb1("ftmp", [P, LC])
        facc = sb1("facc", [P, LC])
        gate_op = sb1("gate_op", [P, 1])
        ang, turns, ve, vo, al, be, ge, go, sn, cs, t1, t2, t3, t4, oe, oo = (
            sb1(name, [HALF, 2, T]) for name in ("ang", "turns", "ve", "vo", "al", "be", "ge", "go", "sn", "cs",
                                                 "t1", "t2", "t3", "t4", "oe", "oo"))
        ab = turns
        rexp = sb1("rexp", [P, NT, HEADS0, PAIRS])
        def split1(name, shape):
            return [sb1(f"{name}_{part}", shape, F32R) for part in ("high", "low")]

        hm2 = split1("hm2", [P, KD, T])
        wgu2 = [split1(f"wgu2{i}", [P, 2 * D]) for i in range(2)]
        wdn2 = [split1(f"wdn2{i}", [P, D]) for i in range(2)]
        act2 = [split1(f"act2{i}", [P, T]) for i in range(2)]
        wgu = [sb1(f"wgu{i}", [P, 2 * D]) for i in range(2)]
        wdn = [sb1(f"wdn{i}", [P, D]) for i in range(2)]
        aff = sb1("aff", [P, NT, NEXP])
        bia = sb1("bia", [P, NT, NEXP])
        r1 = sb1("r1", [P, NT, NEXP])
        r2 = sb1("r2", [P, NT, NEXP])
        m1 = sb1("m1", [P, NT])
        pick = sb1("pick", [P, NT, NEXP])
        mask = sb1("mask", [P, NT, NE])
        sg = [sb1(f"sg{i}", [P, T]) for i in range(2)]
        act = [sb1(f"act{i}", [P, T]) for i in range(2)]
        stage1.close()

        def split(name, shape):
            return [sb(f"{name}_{part}", shape, F32R) for part in ("high", "low")]

        fw2 = split("fw2", [P, FW])
        h2 = split("h2", [P, KD, T])
        f2 = split("f2", [P, KD, T])
        wraw = [sb(f"wraw{i}", [P, 6 * D]) for i in range(2)]
        wraw_o = [sb(f"wraw_o{i}", [P, 2, D]) for i in range(2)]
        wqk2 = [split(f"wqk{i}", [P, 2, KD, DH]) for i in range(2)]
        wv2 = [split(f"wv{i}", [P, KD, 2 * DH]) for i in range(2)]
        wo2 = [split(f"wo{i}", [P, D]) for i in range(2)]
        q2 = split("q2", [P, T])
        k2 = split("k2", [P, T])
        v2 = [split(f"v2{i}", [P, NT, 2, DH]) for i in range(2)]
        pr = sb("pr", [P, NT, T])
        p2 = split("p2", [P, 3, T])
        z2 = split("z2", [P, T])
        negmax = sb("negmax", [P, NT])
        rsum = sb("rsum", [P, NT])
        rinv = sb("rinv", [P, NT])
        fsg = [sb(f"fsg{i}", [P, T]) for i in range(2)]
        ft = [sb(f"ft{i}", [P, T]) for i in range(2)]
        fa2 = split("fa2", [P, NM, T])

        def ffn_weights(part):
            w = fw2[part]
            return (w[:, 0:KD * INTER_PAD].rearrange("p (k n) -> p k n", k=KD),
                    w[:, KD * INTER_PAD:2 * KD * INTER_PAD].rearrange("p (k n) -> p k n", k=KD),
                    w[:, 2 * KD * INTER_PAD:].rearrange("p (m n) -> p m n", m=NM))

        s_const = sem("consts_loaded")
        s_made = sem("consts_made")
        s_made2 = sem("consts_selected")
        s_setup = sem("setup_by_vector")
        s_pad = sem("extra_batch_stored")
        s_x0 = sem("x_loaded_stage1")
        s_x0free = sem("x_taken_stage1")
        s_x1 = sem("x_loaded_stage2")
        s_x1free = sem("x_taken_stage2")
        s_st1 = sem("x1_stored")
        s_st2 = sem("out_stored")
        s_kept1 = sem("residual_stored_stage1")
        s_xn = [sem(f"ln{n}_normalised") for n in range(4)]
        s_hTp = [sem(f"ln{n}_transposed") for n in range(4)]
        s_hTa = [sem(f"ln{n}_copied_by_scalar") for n in range(4)]
        s_hTv = [sem(f"ln{n}_copied_by_vector") for n in range(4)]
        s_lnc = [sem(f"ln{n}_chain") for n in range(4)]
        s_xdone = [sem(f"sublayer{n}_added") for n in range(4)]
        s_pv = sem("l0_projected_for_vector")
        s_pa = sem("l0_projected_for_scalar")
        s_cv = sem("l0_conv_done")
        s_ga = sem("l0_gates_read")
        s_ab = sem("l0_alpha_beta")
        s_rng = sem("l0_angle_reduced")
        s_abs = sem("l0_angle_abs")
        s_trig = sem("l0_sin_cos")
        s_scan = sem("l0_scanned")
        s_sq = sem("l0_squares")
        s_ms = sem("l0_square_sums")
        s_re = sem("l0_rms_spread")
        s_rT = sem("l0_rms_transposed")
        s_y = sem("l0_gated")
        s_o0 = sem("l0_out_product")
        s_l0 = sem("l0_chain")
        s_lg = sem("router_logits")
        s_lgc = sem("router_logits_clamped")
        s_ex = sem("router_exp")
        s_mask = sem("router_mask")
        s_rc = sem("router_chain")
        s_w = [sem(f"expert_gate_up_weights{i}") for i in range(2)]
        s_wd = [sem(f"expert_down_weights{i}") for i in range(2)]
        s_wgh = sem("expert_gate_up_weights_high")
        s_wgl = sem("expert_gate_up_weights_split")
        s_wdh = sem("expert_down_weights_high")
        s_wdl = sem("expert_down_weights_split")
        s_mh = sem("moe_input_high")
        s_ml = sem("moe_input_split")
        s_ah = sem("expert_activation_high")
        s_al = sem("expert_activation_split")
        s_gu = sem("expert_gate_product")
        s_up = sem("expert_up_product")
        s_silu = sem("expert_silu")
        s_act = sem("expert_activation")
        s_dn = sem("expert_down_product")
        s_acc = sem("expert_added")
        s_facc = sem("ffn_weights_moved")
        s_fidx = sem("ffn_indices_loaded")
        s_lut = sem("lut_chain")
        s_wr = [sem(f"head_weights_loaded{i}") for i in range(2)]
        s_wro = [sem(f"out_weights_loaded{i}") for i in range(2)]
        s_wrv = [sem(f"v_weights_loaded{i}") for i in range(2)]
        s_wqh = sem("head_qk_weights_high")
        s_wvh = sem("pair_v_weights_high")
        s_wv = sem("pair_v_weights_split")
        s_woh = sem("head_out_weights_high")
        s_wq = sem("head_qk_weights_split")
        s_wo = sem("head_out_weights_split")
        s_q = sem("q_product")
        s_k = sem("k_product")
        s_v = sem("v_half_product")
        s_qh = sem("q_high")
        s_ql = sem("q_split")
        s_kh = sem("k_high")
        s_kl = sem("k_split")
        s_vh = sem("v_high")
        s_vl = sem("v_split")
        s_s = sem("scores_bank")
        s_mx = sem("score_max_bank")
        s_e = sem("exps")
        s_t = sem("probs_transposed_bank")
        s_ph = sem("probs_high_bank")
        s_pl = sem("probs_split_bank")
        s_z = sem("z_product")
        s_zh = sem("z_high")
        s_zl = sem("z_split")
        s_o = sem("out_product_bank")
        s_ob = sem("out_product_added")
        s_ri = sem("row_sum_inverted")
        s_fwh = sem("ffn_weights_high")
        s_fw = sem("ffn_weights_split")
        s_fg = sem("ffn_gate_product")
        s_fu = sem("ffn_up_product")
        s_fs = sem("ffn_silu")
        s_fm = sem("ffn_activation")
        s_fh = sem("ffn_activation_high")
        s_fa = sem("ffn_activation_split")
        s_fd = sem("ffn_down_product")

        CONST_DMAS = 11
        block = ctx.enter_context(nc.Block())

        def rows(ap):
            return ap.rearrange("(n p) d -> p n d", p=P)

        SCORE_BANKS = ((0, 2), (1,), (3,))
        PROB_TILES = ((0,), (1, 3), (2,))
        PROB_COLS = (4 * P, 4 * P, 2 * P)

        def score(i):
            if i == 0:
                return bank[2][:, 3 * P:4 * P]
            return bank[{2: 2, 1: 3, 3: 4}[i]][:, 0:(i + 1) * P]

        def prob_at(j):
            return ((0, 0), (1, 0), (2, 0), (1, 3 * P))[j]

        @block.sync
        def _(sp):
            for dst, src in ((w0s, w0), (wabs, wab), (cws, cw), (invfs, invf), (rmsws, rmsw), (wo0s, wo0),
                             (cents, cent), (gbiass, gbias), (iotas, iota16), (lutks, lutk), (luts, lut)):
                sp.dma_start(dst[:], src).then_inc(s_const, 16)

            sp.dma_start(x1[NB, :, :], x_in[0, :, :]).then_inc(s_pad, 16)

            def load_experts(b, i):
                for p in range(2):
                    w = wexp[bass.ds(2 * i + p, 1), :, :].rearrange("a p n -> (a p) n")
                    gate_up_w, down_w = w[:, 0:2 * D], w[:, 2 * D:]
                    sp.wait_ge(s_wgl, b * NE + 2 * i + (p - 1 + 2 * START))
                    sp.dma_start(wgu[p][:], gate_up_w).then_inc(s_w[p], 16)
                    sp.wait_ge(s_wdl, b * NE + 2 * i + (p - 1 + 2 * START))
                    sp.dma_start(wdn[p][:], down_w).then_inc(s_wd[p], 16)

            sp.dma_start(xin[:], rows(x_in[0, :, :])).then_inc(s_x0, 16)
            with sp.Fori(0, NB) as b:
                indices = fidx[bass.ds(b, 1), :, :].rearrange("a p n -> (a p) n")
                sp.wait_ge(s_lut, LUT_STEPS * LUTN * b + START)
                sp.dma_start(fidxs[:], indices).then_inc(s_fidx, 16)
                load_experts(b, 0)
                next_x = rows(x_in[bass.ds(b + 1, 1), :, :].rearrange("a t d -> (a t) d"))
                sp.wait_ge(s_x0free, b + 1)
                sp.dma_start(xin[:], next_x).then_inc(s_x0, 16)
                with sp.Fori(1, NE // 2) as i:
                    load_experts(b, i)
            sp.wait_ge(s_st1, 16 * NB)
            sp.wait_ge(s_pad, 16)

            def pair_weights(p, w):
                return ((s_wr[p], wraw[p][:, 0:4 * D], w[:, 0:4 * D]),
                        (s_wrv[p], wraw[p][:, 4 * D:6 * D], w[:, 4 * D:6 * D]),
                        (s_wro[p], wraw_o[p][:].rearrange("p h d -> p (h d)"), w[:, 6 * D:]))

            def reload_pair(n, p, w):
                qk, v_, o = pair_weights(p, w)
                sp.wait_ge(s_wq, 2 * n - 2)
                sp.dma_start(qk[1], qk[2]).then_inc(qk[0], 16)
                sp.wait_ge(s_wv, n - 1)
                sp.dma_start(v_[1], v_[2]).then_inc(v_[0], 16)
                sp.wait_ge(s_wo, 2 * n - 2)
                sp.dma_start(o[1], o[2]).then_inc(o[0], 16)

            sp.dma_start(xin[:], rows(x1[0, :, :])).then_inc(s_x1, 16)
            for p in range(2):
                for loaded, dst, src in pair_weights(p, wpair[p]):
                    sp.dma_start(dst, src).then_inc(loaded, 16)
            with sp.Fori(0, NB) as b:
                next_x = rows(x1[bass.ds(b + 1, 1), :, :].rearrange("a t d -> (a t) d"))
                sp.wait_ge(s_x1free, b + 1)
                sp.dma_start(xin[:], next_x).then_inc(s_x1, 16)
                with sp.Fori(1, NPAIR // 2) as i:
                    for p in range(2):
                        reload_pair(b * NPAIR + 2 * i + p, p,
                                    wpair[bass.ds(2 * i + p, 1), :, :].rearrange("a p n -> (a p) n"))
                for p in range(2):
                    reload_pair(b * NPAIR + (NPAIR + p), p, wpair[p])
            for p in range(2):
                for loaded in (s_wr, s_wrv, s_wro):
                    sp.wait_ge(loaded[p], 16 * (NB * NPAIR // 2 + 1))

        @block.gpsimd
        def _(pool):
            for s, n in ((s_kept1, 1), (s_wgl, 2), (s_wdl, 2)):
                pool.sem_inc(s, n * START)
            pool.memset(ident[:], 0.0).then_inc(s_made, 1)
            pool.memset(ident_bf[:], 0.0).then_inc(s_made, 1)
            pool.memset(causal[:], 0.0).then_inc(s_made, 1)
            pool.memset(half_pi[:], math.pi / 2).then_inc(s_made, 1)
            pool.memset(headsum[:], 1.0).then_inc(s_made, 1)
            pool.wait_ge(s_made, 5)
            for m in (ident, ident_bf):
                pool.affine_select(out=m[:], in_=m[:], compare_op=ALU.not_equal, fill=1.0, base=0,
                                   pattern=[[-1, P]], channel_multiplier=1).then_inc(s_made2, 1)
            pool.affine_select(out=causal[:], in_=causal[:], compare_op=ALU.is_ge, fill=NEG, base=0,
                               pattern=[[-1, P]], channel_multiplier=1).then_inc(s_made2, 1)
            pool.affine_select(out=headsum[:], in_=headsum[:], compare_op=ALU.is_ge, fill=0.0, base=0,
                               pattern=[[-PAIRS, 3]], channel_multiplier=1).then_inc(s_made2, 1)
            pool.wait_ge(s_made2, 4)
            pool.affine_select(out=headsum[:], in_=headsum[:], compare_op=ALU.is_ge, fill=0.0, base=PAIRS - 1,
                               pattern=[[PAIRS, 3]], channel_multiplier=-1).then_inc(s_made2, 1)
            pool.sem_inc(s_lut, START)
            pool.wait_ge(s_const, 16 * CONST_DMAS)
            with pool.Fori(0, NB) as b:
                def low_gate_up(e, p):
                    pool.wait_ge(s_wgh, b * NE + e + 1)
                    pool.tensor_tensor(wgu2[p][1][:], wgu[p][:], wgu2[p][0][:].bitcast(F32), ALU.subtract
                                       ).then_inc(s_wgl, 1)

                def low_down(e, p):
                    pool.wait_ge(s_wdh, b * NE + e + 1)
                    pool.tensor_tensor(wdn2[p][1][:], wdn[p][:], wdn2[p][0][:].bitcast(F32), ALU.subtract
                                       ).then_inc(s_wdl, 1)

                low_gate_up(0, 0)
                low_gate_up(1, 1)
                low_down(0, 0)
                pool.wait_ge(s_fidx, (b + 1) * 16)
                for e in range(LUTN):
                    n = LUT_STEPS * (b * LUTN + e) + START
                    if e == 0:
                        pool.wait_ge(s_facc, b + START)
                    pool.wait_ge(s_lut, n)
                    pool.tensor_tensor(gate_op[:], ident[:, 0:1], ident[:, 0:1], ALU.subtract)
                    if e == 0:
                        pool.tensor_scalar(facc[:], fidxs[:], lutks[:, e:e + 1], luts[:, e:e + 1], ALU.is_equal,
                                           ALU.mult).then_inc(s_lut, LUT_STEPS)
                    else:
                        pool.tensor_scalar(ftmp[:], fidxs[:], lutks[:, e:e + 1], luts[:, e:e + 1], ALU.is_equal,
                                           ALU.mult).then_inc(s_lut, 1)
                        pool.wait_ge(s_lut, n + 1)
                        pool.tensor_tensor(facc[:], facc[:], ftmp[:], ALU.add).then_inc(s_lut, 1)
                for k in range(KD):
                    pool.wait_ge(s_mh, b * KD + k + 1)
                    pool.tensor_tensor(hm2[1][:, k, :], hT[:, k, :], hm2[0][:, k, :].bitcast(F32), ALU.subtract
                                       ).then_inc(s_ml, 1)
                low_down(1, 1)
                low_gate_up(2, 0)
                with pool.Fori(0, NE // 2 - 2) as i:
                    for c in range(2):
                        low_gate_up(2 * i + (c + 3), (c + 1) % 2)
                        low_down(2 * i + (c + 2), c)
                low_gate_up(NE - 1, 1)
                low_down(NE - 2, 0)
                low_down(NE - 1, 1)
                pool.wait_ge(s_acc, (b + 1) * NE + START)
                pool.dma_start(rows(x1[bass.ds(b, 1), :, :].rearrange("a t d -> (a t) d")), xr[:]).then_inc(s_st1, 16)
                pool.wait_ge(s_st1, b * 16 + 16)
                pool.sem_inc(s_kept1, 1)
            def low_qk_weights(g, e, r):
                high, low = (w[:].rearrange("p c k n -> p (c k n)") for w in wqk2[e])
                pool.wait_ge(s_wqh, g + 1)
                pool.tensor_tensor(low, wraw[r][:, 2 * e * D:2 * (e + 1) * D], high.bitcast(F32), ALU.subtract
                                   ).then_inc(s_wq, 1)

            def low_v_weights(n, r):
                high, low = (w[:].rearrange("p k n -> p (k n)") for w in wv2[r])
                pool.wait_ge(s_wvh, n + 1)
                pool.tensor_tensor(low, wraw[r][:, 4 * D:6 * D], high.bitcast(F32), ALU.subtract).then_inc(s_wv, 1)

            def low_out_weights(g, e, r):
                pool.wait_ge(s_woh, g + 1)
                pool.tensor_tensor(wo2[e][1][:], wraw_o[r][:, e, :], wo2[e][0][:].bitcast(F32), ALU.subtract
                                   ).then_inc(s_wo, 1)

            low_qk_weights(0, 0, 0)
            low_qk_weights(1, 1, 0)
            low_v_weights(0, 0)
            low_v_weights(1, 1)
            low_out_weights(0, 0, 0)
            with pool.Fori(0, NB * NH // 4) as i:
                for j in range(4):
                    low_out_weights(4 * i + (j + 1), (j + 1) % 2, (j + 1) // 2 % 2)
                    low_qk_weights(4 * i + (j + 2), j % 2, (j + 2) // 2 % 2)
                    if j % 2:
                        low_v_weights(2 * i + (j // 2 + 2), j // 2 % 2)

        @block.scalar
        def _(sc):
            sc.sem_inc(s_st2, 16)
            sc.wait_ge(s_made2, 5)

            def high(dst, src, done, scale=1.0):
                sc.activation(dst, src, ACT.Copy, scale=scale).then_inc(done, 1)

            def layer_norm_copy(n, b):
                sc.wait_ge(s_hTp[n], b + 1)
                for k in range(KD if n == 0 else 1):
                    sc.activation(hT[:, k, :], bank[k][:], ACT.Copy).then_inc(s_hTa[n], 1)

            with sc.Fori(0, NB) as b:
                def high_gate_up(e, p, nload):
                    sc.wait_ge(s_w[p], nload * 16)
                    sc.wait_ge(s_up, b * NE + e - 1 + 2 * START)
                    high(wgu2[p][0][:], wgu[p][:], s_wgh)

                def high_down(e, p, nload):
                    sc.wait_ge(s_wd[p], nload * 16)
                    sc.wait_ge(s_dn, b * NE + e - 1 + 2 * START)
                    high(wdn2[p][0][:], wdn[p][:], s_wdh)

                def nload(i, c):
                    return b * (NE // 2) + (i + (c // 2 + 1))

                layer_norm_copy(0, b)
                high_gate_up(0, 0, nload(0, 0))
                high_gate_up(1, 1, nload(0, 1))
                high_down(0, 0, nload(0, 0))
                for hf in range(2):
                    for j, dst in enumerate((al, be, ge, go)):
                        sc.wait_ge(s_pa, b * 8 + hf * 4 + j + 1)
                        if j < 2:
                            sc.activation(dst[:, hf, :], bank[4 + j][0:HALF, :], ACT.Tanh, scale=0.5).then_inc(s_ga, 1)
                        else:
                            sc.activation(dst[:, hf, :], bank[4 + j][0:HALF, :], ACT.Silu).then_inc(s_ga, 1)
                    for j, dst in enumerate((al, be)):
                        sc.wait_ge(s_ga, b * 8 + hf * 4 + j + 1)
                        sc.activation(dst[:, hf, :], dst[:, hf, :], ACT.Copy, scale=0.5, bias=0.5
                                      ).then_inc(s_ab, 1)
                    sc.wait_ge(s_rng, b * 2 + hf + 1)
                    sc.activation(ab[:, hf, :], ang[:, hf, :], ACT.Abs).then_inc(s_abs, 1)
                    sc.activation(sn[:, hf, :], ang[:, hf, :], ACT.Sin)
                    sc.wait_ge(s_abs, b * 2 + hf + 1)
                    sc.activation(cs[:, hf, :], ab[:, hf, :], ACT.Sin, scale=-1.0, bias=half_pi[0:HALF, :]
                                  ).then_inc(s_trig, 1)
                for hf in range(2):
                    sc.wait_ge(s_scan, b * 2 + hf + 1)
                    sc.activation(sn[:, hf, :], oe[:, hf, :], ACT.Square)
                    sc.activation(cs[:, hf, :], oo[:, hf, :], ACT.Square).then_inc(s_sq, 1)
                layer_norm_copy(1, b)
                for k, copied in enumerate((s_hTa[1], s_hTv[1])):
                    sc.wait_ge(copied, b + 1)
                    high(hm2[0][:, k, :], hT[:, k, :], s_mh)
                sc.wait_ge(s_lgc, b + 1)
                sc.activation(aff[:], bia[:], ACT.Exp, scale=-1.0).then_inc(s_ex, 1)

                def silu_expert(e, p):
                    sc.wait_ge(s_gu, b * NE + e + 1)
                    sc.wait_ge(s_act, b * NE + e - 1 + 2 * START)
                    sc.activation(sg[p][:], bank[p][:], ACT.Silu).then_inc(s_silu, 1)

                def high_act(e, p):
                    sc.wait_ge(s_act, b * NE + e + 1 + 2 * START)
                    sc.wait_ge(s_dn, b * NE + e - 1 + 2 * START)
                    high(act2[p][0][:], act[p][:], s_ah)

                silu_expert(0, 0)
                silu_expert(1, 1)
                high_down(1, 1, nload(0, 1))
                high_gate_up(2, 0, nload(0, 2))
                high_act(0, 0)
                with sc.Fori(0, NE // 2 - 2) as i:
                    for c in range(2):
                        high_act(2 * i + (c + 1), (c + 1) % 2)
                        silu_expert(2 * i + (c + 2), c)
                        high_gate_up(2 * i + (c + 3), (c + 1) % 2, nload(i, c + 3))
                        high_down(2 * i + (c + 2), c, nload(i, c + 2))
                high_act(NE - 3, 1)
                silu_expert(NE - 2, 0)
                high_gate_up(NE - 1, 1, nload(0, NE - 1))
                high_down(NE - 2, 0, nload(0, NE - 2))
                high_act(NE - 2, 0)
                silu_expert(NE - 1, 1)
                high_down(NE - 1, 1, nload(0, NE - 1))
                high_act(NE - 1, 1)

            def layer_norm_high(n, b, dst, bank0):
                sc.wait_ge(s_hTp[n], b + 1)
                for k in range(KD):
                    high(dst[0][:, k, :], bank[bank0 + k][:], s_hTa[n])

            def high_qk(g):
                sc.wait_ge(s_q, g + 1)
                high(q2[0][:], bank[0][:], s_qh, SCALE)
                sc.wait_ge(s_k, g + 1 + 2 * START)
                high(k2[0][:], bank[1][:], s_kh)

            def high_v(c, r, half, src):
                sc.wait_ge(s_v, c + 1 + 3 * START)
                high(v2[r][0][:, 2 * half:2 * half + 2].rearrange("p t h n -> p (t h n)"), src, s_vh)

            def high_qk_weights(g, e, r, nload):
                sc.wait_ge(s_wr[r], nload * 16)
                sc.wait_ge(s_k, g - 1 + 2 * START)
                high(wqk2[e][0][:].rearrange("p c k n -> p (c k n)"), wraw[r][:, 2 * e * D:2 * (e + 1) * D], s_wqh)

            def high_v_weights(n, r, nload):
                sc.wait_ge(s_wrv[r], nload * 16)
                sc.wait_ge(s_v, 2 * n - 2 + 3 * START)
                high(wv2[r][0][:].rearrange("p k n -> p (k n)"), wraw[r][:, 4 * D:6 * D], s_wvh)

            def high_out_weights(g, e, r, nload):
                sc.wait_ge(s_wro[r], nload * 16)
                sc.wait_ge(s_o, 2 * g - 2 + 3 * START)
                high(wo2[e][0][:], wraw_o[r][:, e, :], s_woh)

            def open_batch(b):
                layer_norm_high(2, b, h2, 0)
                high_qk(b * NH)
                high_v(b * NH, 0, 0, bank[5][:])
                high_v(b * NH + 1, 0, 1, bank[2][:])

            sc.wait_ge(s_st1, 16 * NB)
            high_qk_weights(0, 0, 0, 1)
            high_qk_weights(1, 1, 0, 1)
            high_v_weights(0, 0, 1)
            high_v_weights(1, 1, 1)
            high_out_weights(0, 0, 0, 1)
            open_batch(0)
            sc.wait_ge(s_facc, NB + START)
            high(fw2[0][:], fws[:], s_fwh)
            with sc.Fori(0, NB) as b:
                def softmax(g):
                    for n, tiles in enumerate(SCORE_BANKS):
                        sc.wait_ge(s_mx, 3 * g + n + 1)
                        for i in tiles:
                            ins = sc.activation(pr[:, i, 0:(i + 1) * P], score(i), ACT.Exp, bias=negmax[:, i:i + 1],
                                                accum_out=rsum[:, i:i + 1])
                    ins.then_inc(s_e, 1)

                def high_probs(g):
                    for n in range(3):
                        sc.wait_ge(s_t, 3 * g + n + 1)
                        high(p2[0][:, n, 0:PROB_COLS[n]], bank[2 + n][:, 0:PROB_COLS[n]], s_ph)

                def high_z(g):
                    sc.wait_ge(s_z, g + 1)
                    high(z2[0][:], bank[0][:], s_zh)

                def head(i, j, last_pair=False, last=False):
                    g = b * NH + (4 * i + j)

                    def nload(pairs_on):
                        return b * (NPAIR // 2) + (i + (pairs_on // 2 + 1))

                    softmax(g)
                    if not last:
                        high_qk(g + 1)
                    on = (j + 1) // 2
                    high_out_weights(g + 1, (j + 1) % 2, on % 2, nload(on))
                    high_probs(g)
                    if not last_pair:
                        high_v(g + 2, (j // 2 + 1) % 2, j % 2, bank[5][:])
                    on = (j + 2) // 2
                    high_qk_weights(g + 2, j % 2, on % 2, nload(on))
                    if j % 2:
                        on = j // 2 + 2
                        high_v_weights(b * NPAIR + (2 * i + on), on % 2, nload(on))
                    high_z(g)

                with sc.Fori(0, QUADS) as i:
                    for j in range(4):
                        head(i, j)
                for j in range(4):
                    head(QUADS, j, last_pair=j >= 2, last=j == 3)
                open_batch(b + 1)
                layer_norm_high(3, b, f2, 3)

                def silu(m):
                    sc.wait_ge(s_fg, b * NM + m + 1)
                    if m >= 2:
                        sc.wait_ge(s_fm, b * NM + m - 1)
                    sc.activation(fsg[m % 2][:], bank[m % 2][:], ACT.Silu).then_inc(s_fs, 1)

                silu(0)
                for m in range(NM):
                    if m + 1 < NM:
                        silu(m + 1)
                    sc.wait_ge(s_fm, b * NM + m + 1)
                    high(fa2[0][:, m, :], ft[m % 2][:], s_fh)
                sc.wait_ge(s_xdone[3], b + 1 + START)
                sc.dma_start(rows(out[bass.ds(b, 1), :, :].rearrange("a t d -> (a t) d")), xr[:]).then_inc(s_st2, 16)
            sc.wait_ge(s_st2, 16 * NB + 16)

        @block.vector
        def _(v):
            for s, n in ((s_acc, 1), (s_ob, 1), (s_xdone[3], 1), (s_act, 2), (s_al, 2), (s_facc, 1)):
                v.sem_inc(s, n * START)
            v.wait_ge(s_const, 16 * CONST_DMAS)
            v.memset(mask[:], SHARED_RATIO).then_inc(s_setup, 1)
            for k in range(KD):
                for j in range(2):
                    v.tensor_copy(wabr[:, k, j].rearrange("p h (a c) -> p (h a) c", c=PAIRS),
                                  wabs[:, k, j, :].unsqueeze(2).to_broadcast([P, HEADS0, PAIRS]))
            v.tensor_scalar(cws[:, 0], cws[:, 0], invfs[:, 0:1], -1.0, ALU.mult, ALU.mult)
            v.tensor_scalar(cws[:, 1], cws[:, 1], invfs[:, 0:1], None, ALU.mult).then_inc(s_setup, 1)
            v.wait_ge(s_setup, 2)

            def rsqrt(n, link, extra):
                link(v.tensor_scalar(ry[:, 0:n].bitcast(I32), va[:, 0:n].bitcast(I32), -0.5, RSQRT_SEED,
                                     ALU.mult, ALU.add))
                for _ in range(3):
                    link(v.tensor_tensor(rt[:, 0:n], ry[:, 0:n], ry[:, 0:n], ALU.mult))
                    link(v.scalar_tensor_tensor(rt[:, 0:n], rt[:, 0:n], -0.5, va[:, 0:n], ALU.mult, ALU.mult))
                    link(v.scalar_tensor_tensor(ry[:, 0:n], rt[:, 0:n], 1.5, ry[:, 0:n], ALU.add, ALU.mult))

            def layer_norm(n, b, src):
                done = [0]

                def link(ins):
                    done[0] += 1
                    ins.then_inc(s_lnc[n], 1)
                    v.wait_ge(s_lnc[n], b * LN_LINKS + done[0])

                for i in range(NT):
                    ins = v.bn_stats(stats[:, i, :], src[:, i, :])
                link(ins)
                v.tensor_tensor(mv[:, :, 0], stats[:, :, 1], stats[:, :, 4], ALU.add)
                v.tensor_tensor(rt[:, 0:NT], stats[:, :, 1], stats[:, :, 4], ALU.subtract)
                link(v.tensor_tensor(mv[:, :, 1], stats[:, :, 2], stats[:, :, 5], ALU.add))
                v.tensor_scalar(mv[:, :, 0], mv[:, :, 0], 0.5, None, ALU.mult)
                v.tensor_scalar(mv[:, :, 1], mv[:, :, 1], 1.0 / D, EPS, ALU.mult, ALU.add)
                link(v.tensor_tensor(rt[:, 0:NT], rt[:, 0:NT], rt[:, 0:NT], ALU.mult))
                link(v.scalar_tensor_tensor(va[:, 0:NT], rt[:, 0:NT], 0.25, mv[:, :, 1], ALU.mult, ALU.add))
                rsqrt(NT, link, 0)
                assert done[0] == LN_LINKS
                if n == 3:
                    v.wait_ge(s_hTp[2], b + 2)
                for i in range(NT):
                    ins = v.tensor_scalar(xn[:, i, :], src[:, i, :], mv[:, i, 0:1], ry[:, i:i + 1],
                                          ALU.subtract, ALU.mult)
                ins.then_inc(s_xn[n], 1)

            def layer_norm_copy(b):
                v.wait_ge(s_hTp[1], b + 1)
                v.tensor_copy(hT[:, 1, :], bank[1][:]).then_inc(s_hTv[1], 1)

            def layer_norm_low(n, b, dst, bank0):
                for k in range(KD):
                    v.wait_ge(s_hTa[n], b * KD + k + 1)
                    low(dst, bank[bank0 + k][:], s_hTv[n], lambda part: part[:, k, :])

            def low(parts, src, done, at=lambda part: part[:], scale=None):
                high_ = at(parts[0]).bitcast(F32)
                if scale is None:
                    v.tensor_tensor(at(parts[1]), src, high_, ALU.subtract).then_inc(done, 1)
                else:
                    v.scalar_tensor_tensor(at(parts[1]), src, scale, high_, ALU.mult, ALU.subtract).then_inc(done, 1)

            v.wait_ge(s_x0, 16)
            layer_norm(0, 0, xin)
            with v.Fori(0, NB) as b:
                done = [0]

                def link(ins):
                    done[0] += 1
                    ins.then_inc(s_l0, 1)
                    v.wait_ge(s_l0, b * L0_LINKS + done[0])

                def conv_tile(n, dst, hf, quant, first):
                    v.wait_ge(s_pv, b * 8 + n + 1)
                    src = bank[n % 4][0:HALF, :]
                    tap = [cws[:, quant, hf, j:j + 1] for j in range(TAPS)]
                    d = dst[:, hf, :]
                    if first:
                        link(v.tensor_scalar(d, src, tap[TAPS - 1], None, ALU.mult))
                    else:
                        link(v.scalar_tensor_tensor(d, src, tap[TAPS - 1], d, ALU.mult, ALU.add))
                    for s in range(1, TAPS):
                        ins = v.scalar_tensor_tensor(d[:, s:T], src[:, 0:T - s], tap[TAPS - 1 - s], d[:, s:T],
                                                     ALU.mult, ALU.add)
                        if s < TAPS - 1:
                            link(ins)
                    ins.then_inc(s_cv, 1)
                    v.wait_ge(s_cv, b * 8 + n + 1)

                for hf in range(2):
                    conv_tile(4 * hf + 0, ang, hf, 0, True)
                    conv_tile(4 * hf + 1, ang, hf, 1, False)
                    a, n_ = ang[:, hf, :], turns[:, hf, :]
                    link(v.tensor_scalar(n_, a, 1.0 / TWO_PI, ROUND, ALU.mult, ALU.add))
                    link(v.tensor_scalar(n_, n_, ROUND, None, ALU.subtract))
                    link(v.scalar_tensor_tensor(a, n_, -PI_HI, a, ALU.mult, ALU.add))
                    link(v.scalar_tensor_tensor(a, n_, -PI_LO, a, ALU.mult, ALU.add))
                    v.tensor_scalar(a, a, PI_MAX, -PI_MAX, ALU.min, ALU.max).then_inc(s_rng, 1)
                    conv_tile(4 * hf + 2, ve, hf, 2, True)
                    conv_tile(4 * hf + 3, vo, hf, 3, True)
                for hf in range(2):
                    v.wait_ge(s_trig, b * 2 + hf + 1)
                    v.wait_ge(s_ab, b * 4 + 2 * hf + 2)
                    h = (slice(None), hf, slice(None))
                    v.tensor_tensor(cs[h], cs[h], be[h], ALU.mult)
                    link(v.tensor_tensor(sn[h], sn[h], be[h], ALU.mult))
                    v.tensor_tensor(t1[h], ve[h], cs[h], ALU.mult)
                    v.tensor_tensor(t2[h], vo[h], sn[h], ALU.mult)
                    v.tensor_tensor(t3[h], vo[h], cs[h], ALU.mult)
                    link(v.tensor_tensor(t4[h], ve[h], sn[h], ALU.mult))
                    v.tensor_tensor(t1[h], t1[h], t2[h], ALU.subtract)
                    link(v.tensor_tensor(t3[h], t3[h], t4[h], ALU.add))
                    v.tensor_tensor_scan(oe[h], al[h], t1[h], 0.0, ALU.mult, ALU.add)
                    v.tensor_tensor_scan(oo[h], al[h], t3[h], 0.0, ALU.mult, ALU.add).then_inc(s_scan, 1)
                v.wait_ge(s_scan, b * 2 + 2)
                v.wait_ge(s_ga, b * 8 + 8)
                for hf in range(2):
                    h = (slice(None), hf, slice(None))
                    v.scalar_tensor_tensor(ge[h], ge[h], rmsws[:, 0:1], oe[h], ALU.mult, ALU.mult)
                    ins = v.scalar_tensor_tensor(go[h], go[h], rmsws[:, 1:2], oo[h], ALU.mult, ALU.mult)
                link(ins)
                v.wait_ge(s_ms, b + 1)
                link(v.tensor_scalar(va[:], bank[2][:, 0:NT * HEADS0], 1.0 / (2 * PAIRS), EPS, ALU.mult, ALU.add))
                rsqrt(NT * HEADS0, link, 0)
                v.tensor_copy(rexp[:].rearrange("p t h c -> p (t h) c"),
                              ry[:].unsqueeze(2).to_broadcast([P, NT * HEADS0, PAIRS])).then_inc(s_re, 1)
                v.wait_ge(s_rT, b + 1)
                for hf in range(2):
                    h = (slice(None), hf, slice(None))
                    v.tensor_tensor(ge[h], ge[h], bank[4 + hf][0:HALF, :], ALU.mult)
                    ins = v.tensor_tensor(go[h], go[h], bank[4 + hf][0:HALF, :], ALU.mult)
                ins.then_inc(s_y, 1)
                assert done[0] == L0_LINKS, done[0]
                v.wait_ge(s_o0, b + 1)
                v.wait_ge(s_kept1, b + START)
                for i in range(2):
                    ins = v.tensor_tensor(xr[:, 2 * i:2 * i + 2, :].rearrange("p n d -> p (n d)"), bank[6 + i][:],
                                          xin[:, 2 * i:2 * i + 2, :].rearrange("p n d -> p (n d)"), ALU.add)
                ins.then_inc(s_x0free, 1)
                v.wait_ge(s_x0free, b + 1)

                layer_norm(1, b, xr)
                layer_norm_copy(b)
                rdone = [0]

                def rlink(ins):
                    rdone[0] += 1
                    ins.then_inc(s_rc, 1)
                    v.wait_ge(s_rc, b * RC_LINKS + rdone[0])

                v.wait_ge(s_lg, b + 1)
                v.tensor_scalar(bia[:], bank[2][:, 0:NT * NEXP].rearrange("p (t e) -> p t e", t=NT), -87.0, None,
                                ALU.max).then_inc(s_lgc, 1)
                v.wait_ge(s_ex, b + 1)
                rlink(v.tensor_scalar(r1[:], aff[:], 1.0, None, ALU.add))
                rlink(v.reciprocal(aff[:], r1[:]))
                rlink(v.tensor_tensor(bia[:], aff[:], gbiass[:], ALU.add))
                for turn in range(2):
                    rlink(v.tensor_reduce(m1[:], bia[:], AX_X, ALU.max))
                    rlink(v.tensor_tensor(r1[:], bia[:], m1[:].unsqueeze(2).to_broadcast([P, NT, NEXP]), ALU.is_lt))
                    rlink(v.scalar_tensor_tensor(r1[:].rearrange("p t e -> p (t e)"),
                                                 r1[:].rearrange("p t e -> p (t e)"), float(NE),
                                                 iotas[:].rearrange("p t e -> p (t e)"), ALU.mult, ALU.add))
                    rlink(v.tensor_reduce(m1[:], r1[:], AX_X, ALU.min))
                    dst = pick if turn == 0 else r2
                    rlink(v.tensor_tensor(dst[:], iotas[:], m1[:].unsqueeze(2).to_broadcast([P, NT, NEXP]),
                                          ALU.is_equal))
                    if turn == 0:
                        rlink(v.scalar_tensor_tensor(bia[:].rearrange("p t e -> p (t e)"),
                                                     pick[:].rearrange("p t e -> p (t e)"), -3.0e38,
                                                     bia[:].rearrange("p t e -> p (t e)"), ALU.mult, ALU.add))
                rlink(v.tensor_tensor(pick[:], pick[:], r2[:], ALU.add))
                rlink(v.tensor_tensor(pick[:], pick[:], aff[:], ALU.mult))
                rlink(v.tensor_reduce(m1[:], pick[:], AX_X, ALU.add))
                rlink(v.tensor_scalar(m1[:], m1[:], 1e-9, None, ALU.add))
                rlink(v.reciprocal(m1[:], m1[:]))
                assert rdone[0] == RC_LINKS, rdone[0]
                v.tensor_tensor(mask[:, :, 0:NEXP], pick[:], m1[:].unsqueeze(2).to_broadcast([P, NT, NEXP]),
                                ALU.mult).then_inc(s_mask, 1)
                v.wait_ge(s_mask, b + 1)

                def activate(g, p):
                    v.wait_ge(s_silu, g + 1)
                    v.wait_ge(s_up, g + 1 + 2 * START)
                    v.wait_ge(s_al, g - 1 + 2 * START)
                    v.tensor_tensor(act[p][:], sg[p][:], bank[2 + p][:], ALU.mult).then_inc(s_act, 1)
                    v.wait_ge(s_ah, g + 1)
                    low(act2[p], act[p][:], s_al)

                def accumulate(g, e, p):
                    v.wait_ge(s_dn, g + 1 + 2 * START)
                    v.wait_ge(s_acc, g + START)
                    for i in range(NT):
                        ins = v.scalar_tensor_tensor(xr[:, i, :], bank[4 + 2 * p + i // 2][:, (i % 2) * D:(i % 2 + 1) * D],
                                                     mask[:, i, bass.ds(e, 1)], xr[:, i, :], ALU.mult, ALU.add)
                    ins.then_inc(s_acc, 1)

                activate(b * NE, 0)
                with v.Fori(0, NE - 2, 2) as e:
                    for p in range(2):
                        g = b * NE + e + p
                        activate(g + 1, 1 - p)
                        accumulate(g, e + p, p)
                activate(b * NE + NE - 1, 1)
                v.wait_ge(s_x0, (b + 2) * 16)
                layer_norm(0, b + 1, xin)
                accumulate(b * NE + NE - 2, NE - 2, 0)
                accumulate(b * NE + NE - 1, NE - 1, 1)
                v.wait_ge(s_lut, LUT_STEPS * LUTN * (b + 1) + START)
                v.tensor_scalar(fws[:, bass.ds(b * LC, LC)], facc[:], 1.0, None, ALU.mult).then_inc(s_facc, 1)

            def low_qk(g):
                v.wait_ge(s_qh, g + 1)
                low(q2, bank[0][:], s_ql, scale=SCALE)
                v.wait_ge(s_kh, g + 1)
                low(k2, bank[1][:], s_kl)

            def low_v(c, r, half, src):
                v.wait_ge(s_vh, c + 1)
                low(v2[r], src, s_vl, lambda part: part[:, 2 * half:2 * half + 2].rearrange("p t h n -> p (t h n)"))

            def open_batch(b):
                low_qk(b * NH)
                low_v(b * NH, 0, 0, bank[5][:])
                low_v(b * NH + 1, 0, 1, bank[2][:])

            v.wait_ge(s_st1, 16 * NB)
            v.wait_ge(s_facc, NB + START)
            v.wait_ge(s_x1, 16)
            layer_norm(2, 0, xin)
            layer_norm_low(2, 0, h2, 0)
            open_batch(0)
            v.wait_ge(s_fwh, 1)
            low(fw2, fws[:], s_fw)
            with v.Fori(0, NB) as b:
                def score_max(g):
                    for n, tiles in enumerate(SCORE_BANKS):
                        v.wait_ge(s_s, 3 * g + n + 1)
                        for i in tiles:
                            ins = v.tensor_reduce(negmax[:, i:i + 1], score(i), AX_X, ALU.max, negate=True)
                        ins.then_inc(s_mx, 1)

                def low_probs(g):
                    for n in range(3):
                        v.wait_ge(s_ph, 3 * g + n + 1)
                        low(p2, bank[2 + n][:, 0:PROB_COLS[n]], s_pl, lambda part: part[:, n, 0:PROB_COLS[n]])

                def low_z(g):
                    v.wait_ge(s_zh, g + 1)
                    low(z2, bank[0][:], s_zl)

                def invert_sums(g):
                    v.wait_ge(s_ob, g + START)
                    v.reciprocal(rinv[:], rsum[:]).then_inc(s_ri, 1)

                def add_out(g):
                    v.wait_ge(s_ri, g + 1)
                    v.wait_ge(s_x1free, b + 1)
                    v.wait_ge(s_ob, g + START)
                    for n in range(2):
                        v.wait_ge(s_o, 2 * g + n + 1 + 3 * START)
                        for i in (2 * n, 2 * n + 1):
                            ins = v.scalar_tensor_tensor(xr[:, i, :], bank[6 + n][:, (i % 2) * D:(i % 2 + 1) * D],
                                                         rinv[:, i:i + 1], xr[:, i, :], ALU.mult, ALU.add)
                    ins.then_inc(s_ob, 1)

                def head(i, j, first=False, last_pair=False, last=False):
                    g = b * NH + (4 * i + j)
                    score_max(g)
                    if not first:
                        add_out(g - 1)
                    if not last:
                        low_qk(g + 1)
                    low_probs(g)
                    invert_sums(g)
                    if not last_pair:
                        low_v(g + 2, (j // 2 + 1) % 2, j % 2, bank[5][:])
                    low_z(g)

                head(0, 0, first=True)
                v.wait_ge(s_st2, b * 16 + 16)
                v.tensor_copy(xr[:], xin[:]).then_inc(s_x1free, 1)
                with v.Fori(0, QUADS) as i:
                    for j in (1, 2, 3, 4):
                        head(i + j // 4, j % 4)
                head(QUADS, 1)
                v.wait_ge(s_x1, (b + 2) * 16)
                layer_norm(2, b + 1, xin)
                head(QUADS, 2, last_pair=True)
                head(QUADS, 3, last_pair=True, last=True)
                add_out(b * NH + NH - 1)
                layer_norm_low(2, b + 1, h2, 0)
                v.wait_ge(s_ob, b * NH + NH + START)
                layer_norm(3, b, xr)
                open_batch(b + 1)
                layer_norm_low(3, b, f2, 3)

                def ffn_product(m):
                    v.wait_ge(s_fs, b * NM + m + 1)
                    v.wait_ge(s_fu, b * NM + m + 1)
                    if m >= 2:
                        v.wait_ge(s_fa, b * NM + m - 1)
                    v.tensor_tensor(ft[m % 2][:], fsg[m % 2][:], bank[2 + m % 2][:], ALU.mult).then_inc(s_fm, 1)

                def ffn_low(m):
                    v.wait_ge(s_fh, b * NM + m + 1)
                    low(fa2, ft[m % 2][:], s_fa, lambda part: part[:, m, :])

                ffn_product(0)
                for m in range(NM):
                    if m + 1 < NM:
                        ffn_product(m + 1)
                    ffn_low(m)
                v.wait_ge(s_fd, b + 1)
                for i in range(2):
                    x2 = xr[:, 2 * i:2 * i + 2, :].rearrange("p n d -> p (n d)")
                    ins = v.tensor_tensor(x2, bank[6 + i][:], x2, ALU.add)
                ins.then_inc(s_xdone[3], 1)

        @block.tensor
        def _(pe):
            mm = pe.matmul
            for s, n in ((s_dn, 2), (s_up, 2), (s_o, 3), (s_v, 3), (s_k, 2)):
                pe.sem_inc(s, n * START)
            pe.wait_ge(s_const, 16 * CONST_DMAS)
            pe.wait_ge(s_made2, 5)
            pe.wait_ge(s_setup, 2)

            def mm3(dst, w, x, start, stop):
                mm(dst, w[0], x[0], start=start, stop=False)
                mm(dst, w[0], x[1], start=False, stop=False)
                return mm(dst, w[1], x[0], start=False, stop=stop)

            def parts(pair, at):
                return [at(t) for t in pair]

            def layer_norm_transpose(n, b, bank0=0):
                pe.wait_ge(s_xn[n], b + 1)
                for k in range(KD):
                    for i in range(NT):
                        ins = pe.transpose(bank[bank0 + k][:, i * P:(i + 1) * P], xn[:, i, k * P:(k + 1) * P],
                                           ident[:])
                ins.then_inc(s_hTp[n], 1)
                pe.wait_ge(s_hTa[n], (b + 1) * (1 if n == 1 else KD))
                if n > 0:
                    pe.wait_ge(s_hTv[n], (b + 1) * (1 if n == 1 else KD))

            def project3(dst, w_at, x):
                for k in range(KD):
                    ins = mm3(dst, [w_at(part, k) for part in range(2)], parts(x, lambda t: t[:, k, :]),
                              k == 0, k == KD - 1)
                return ins

            def project(dst, w):
                for k in range(KD):
                    ins = mm(dst, w(k), hT[:, k, :], start=(k == 0), stop=(k == KD - 1))
                return ins

            with pe.Fori(0, NB) as b:
                layer_norm_transpose(0, b)
                for hf in range(2):
                    def w_of(q):
                        return lambda k: w0s[:, k, q, hf, :]

                    def ab_of(j):
                        return lambda k: wabr[:, k, j, hf, :]

                    plan = [("v", 0, w_of(0)), ("v", 1, w_of(1)), ("a", 0, ab_of(0)), ("a", 1, ab_of(1)),
                            ("v", 2, w_of(2)), ("v", 3, w_of(3)), ("a", 2, w_of(4)), ("a", 3, w_of(5))]
                    for kind, j, w in plan:
                        if hf == 1:
                            pe.wait_ge(s_cv if kind == "v" else s_ga, b * 8 + j + 1)
                        elif (kind, j) == ("a", 0):
                            pe.wait_ge(s_acc, b * NE + START)
                        dst = bank[j if kind == "v" else 4 + j][0:HALF, :]
                        project(dst, w).then_inc(s_pv if kind == "v" else s_pa, 1)
                pe.wait_ge(s_cv, b * 8 + 8)
                for hf in range(2):
                    pe.wait_ge(s_sq, b * 2 + hf + 1)
                    for i in range(NT):
                        dst = bank[2][:, i * HEADS0 + 3 * hf:i * HEADS0 + 3 * hf + 3]
                        mm(dst, sn[:, hf, i * P:(i + 1) * P], headsum[:], start=True, stop=False)
                        ins = mm(dst, cs[:, hf, i * P:(i + 1) * P], headsum[:], start=False, stop=True)
                ins.then_inc(s_ms, 1)
                pe.wait_ge(s_re, b + 1)
                pe.wait_ge(s_ga, b * 8 + 8)
                for hf in range(2):
                    for i in range(NT):
                        ins = pe.transpose(bank[4 + hf][0:HALF, i * P:(i + 1) * P],
                                           rexp[:, i, 3 * hf:3 * hf + 3, :].rearrange("p h c -> p (h c)"), ident[:])
                ins.then_inc(s_rT, 1)
                pe.wait_ge(s_y, b + 1)
                for i in range(NT):
                    dst = bank[6 + i // 2][:, (i % 2) * D:(i % 2 + 1) * D]
                    n = 0
                    for hf in range(2):
                        for par, src in enumerate((ge, go)):
                            ins = mm(dst, src[:, hf, i * P:(i + 1) * P], wo0s[:, hf, par, :], start=(n == 0),
                                     stop=(n == 3))
                            n += 1
                ins.then_inc(s_o0, 1)

                layer_norm_transpose(1, b)
                for i in range(NT):
                    for k in range(KD):
                        ins = mm(bank[2][:, i * NEXP:(i + 1) * NEXP], hT[:, k, i * P:(i + 1) * P], cents[:, k, :],
                                 start=(k == 0), stop=(k == KD - 1))
                ins.then_inc(s_lg, 1)

                def gate_up(g, p, first=False):
                    pe.wait_ge(s_wgl, g + 1 + 2 * START)
                    if first:
                        pe.wait_ge(s_lgc, b + 1)
                        pe.wait_ge(s_ml, b * KD + KD)
                    else:
                        pe.wait_ge(s_silu, g - 1)
                    project3(bank[p][:], lambda part, k: wgu2[p][part][:, k * P:(k + 1) * P], hm2).then_inc(s_gu, 1)
                    if not first:
                        pe.wait_ge(s_act, g - 1 + 2 * START)
                    project3(bank[2 + p][:], lambda part, k: wgu2[p][part][:, D + k * P:D + (k + 1) * P], hm2
                             ).then_inc(s_up, 1)

                def down(g, p):
                    pe.wait_ge(s_wdl, g + 1 + 2 * START)
                    pe.wait_ge(s_al, g + 1 + 2 * START)
                    for i in range(NT):
                        ins = mm3(bank[4 + 2 * p + i // 2][:, (i % 2) * D:(i % 2 + 1) * D],
                                  parts(act2[p], lambda t: t[:, i * P:(i + 1) * P]), parts(wdn2[p], lambda t: t[:]),
                                  True, True)
                    ins.then_inc(s_dn, 1)

                gate_up(b * NE, 0, first=True)
                gate_up(b * NE + 1, 1, first=True)
                down(b * NE, 0)
                with pe.Fori(0, NE // 2 - 1) as i:
                    for p in (1, 0):
                        g = b * NE + 2 * i + (2 - p)
                        gate_up(g + 1, 1 - p)
                        pe.wait_ge(s_acc, g - 1 + START)
                        down(g, p)
                pe.wait_ge(s_acc, b * NE + NE - 2 + START)
                down(b * NE + NE - 1, 1)

            def make_qk(g, e):
                pe.wait_ge(s_wq, g + 1)
                project3(bank[0][:], lambda part, k: wqk2[e][part][:, 0, k, :], h2).then_inc(s_q, 1)
                project3(bank[1][:], lambda part, k: wqk2[e][part][:, 1, k, :], h2).then_inc(s_k, 1)

            def make_v(n, r, half, dst):
                pe.wait_ge(s_wv, n + 1)
                for i in range(2):
                    for k in range(KD):
                        at = (2 * half + i) * P
                        ins = mm3(dst[:, 2 * i * DH:2 * (i + 1) * DH], parts(h2, lambda t: t[:, k, at:at + P]),
                                  parts(wv2[r], lambda t: t[:, k, :]), k == 0, k == KD - 1)
                ins.then_inc(s_v, 1)

            def open_batch(b):
                layer_norm_transpose(2, b)
                make_qk(b * NH, 0)
                pe.wait_ge(s_vl, b * NH)
                make_v(b * NPAIR, 0, 0, bank[5])
                make_v(b * NPAIR, 0, 1, bank[2])

            layer_norm_transpose(2, 0)
            make_qk(0, 0)
            make_v(0, 0, 0, bank[5])
            make_v(0, 0, 1, bank[2])
            pe.wait_ge(s_vl, 2)
            with pe.Fori(0, NB) as b:
                def scores(g):
                    pe.wait_ge(s_ql, g + 1)
                    pe.wait_ge(s_kl, g + 1)
                    for tiles in SCORE_BANKS:
                        for i in tiles:
                            dst = score(i)
                            mm3(dst, parts(q2, lambda t: t[:, i * P:(i + 1) * P]),
                                parts(k2, lambda t: t[:, 0:(i + 1) * P]), True, False)
                            ins = mm(dst[:, i * P:(i + 1) * P], ident_bf[:], causal[:], start=False, stop=True)
                        ins.then_inc(s_s, 1)

                def transpose_probs(g):
                    pe.wait_ge(s_e, g + 1)
                    for tiles in PROB_TILES:
                        for j in tiles:
                            n, c = prob_at(j)
                            for i in range(j, NT):
                                at = c + (i - j) * P
                                ins = pe.transpose(bank[2 + n][:, at:at + P], pr[:, i, j * P:(j + 1) * P], ident[:])
                        ins.then_inc(s_t, 1)

                def make_z(g, i, j):
                    pe.wait_ge(s_vl, b * NH + (4 * i + (2 * (j // 2) + 2)))
                    done = 0
                    for n, tiles in enumerate(PROB_TILES):
                        pe.wait_ge(s_pl, 3 * g + n + 1)
                        for t_ in tiles:
                            n_, c = prob_at(t_)
                            done += 1
                            ins = mm3(bank[0][:, t_ * P:T], parts(v2[j // 2 % 2], lambda t: t[:, t_, j % 2, :]),
                                      parts(p2, lambda t: t[:, n_, c:c + T - t_ * P]), done == 1, done == NT)
                    ins.then_inc(s_z, 1)

                def project_out(g, e):
                    pe.wait_ge(s_wo, g + 1)
                    pe.wait_ge(s_zl, g + 1)
                    pe.wait_ge(s_ob, g + START)
                    for n in range(2):
                        for i in (2 * n, 2 * n + 1):
                            ins = mm3(bank[6 + n][:, (i % 2) * D:(i % 2 + 1) * D],
                                      parts(z2, lambda t: t[:, i * P:(i + 1) * P]), parts(wo2[e], lambda t: t[:]),
                                      True, True)
                        ins.then_inc(s_o, 1)

                def head(i, j, first=False, last_pair=False, last=False):
                    g = b * NH + (4 * i + j)
                    if not first:
                        project_out(g - 1, (j + 1) % 2)
                    if not last:
                        make_qk(g + 1, (j + 1) % 2)
                    transpose_probs(g)
                    if not last_pair:
                        pe.wait_ge(s_vl, g + 2)
                        make_v(b * NPAIR + (2 * i + (j // 2 + 1)), (j // 2 + 1) % 2, j % 2, bank[5])
                    if first:
                        pe.wait_ge(s_xdone[3], b + START)
                    if not last:
                        pe.wait_ge(s_ql, g + 2)
                    make_z(g, i, j)
                    if not last:
                        scores(g + 1)

                scores(b * NH)
                head(0, 0, first=True)
                with pe.Fori(0, QUADS) as i:
                    for j in (1, 2, 3, 4):
                        head(i + j // 4, j % 4)
                head(QUADS, 1)
                head(QUADS, 2, last_pair=True)
                head(QUADS, 3, last_pair=True, last=True)
                project_out(b * NH + NH - 1, 1)

                open_batch(b + 1)
                layer_norm_transpose(3, b, 3)
                pe.wait_ge(s_fw, 1)
                pe.wait_ge(s_ql, b * NH + NH + 1)
                pe.wait_ge(s_kl, b * NH + NH + 1)
                pe.wait_ge(s_vl, b * NH + NH + 2)
                gate, up, down = zip(ffn_weights(0), ffn_weights(1))
                for m in range(NM):
                    m0 = m * P
                    if m >= 2:
                        pe.wait_ge(s_fs, b * NM + m - 1)
                    project3(bank[m % 2][:], lambda part, k: gate[part][:, k, m0:m0 + P], f2).then_inc(s_fg, 1)
                    if m >= 2:
                        pe.wait_ge(s_fm, b * NM + m - 1)
                    project3(bank[2 + m % 2][:], lambda part, k: up[part][:, k, m0:m0 + P], f2).then_inc(s_fu, 1)
                pe.wait_ge(s_fa, b * NM + NM)
                pe.wait_ge(s_ob, b * NH + NH + START)
                for i in range(NT):
                    for m in range(NM):
                        ins = mm3(bank[6 + i // 2][:, (i % 2) * D:(i % 2 + 1) * D],
                                  parts(fa2, lambda t: t[:, m, i * P:(i + 1) * P]), [w[:, m, :] for w in down],
                                  m == 0, m == NM - 1)
                ins.then_inc(s_fd, 1)


_OUT = (NB, T, D)


def kernel(**inputs):
    import concourse.bacc as bacc
    from concourse.bass_utils import run_bass_kernel_spmd

    a = {k: np.asarray(v) for k, v in inputs.items()}

    def halves(w, parity):
        return w[..., parity::2].reshape(*w.shape[:-1], 2, HALF)

    def kt(w):
        return w.reshape(KD, P, -1).transpose(1, 0, 2)

    wq, wk, wv, wg = (a["L0_attn_W" + c] for c in "qkvg")
    w0 = np.stack([halves(wq, 0), halves(wk, 0), halves(wv, 0), halves(wv, 1), halves(wg, 0), halves(wg, 1)], 1)
    w0 = kt(w0.reshape(D, -1)).reshape(P, KD, 6, 2, HALF)
    wab = kt(np.concatenate([a["L0_attn_Wa"], a["L0_attn_Wb"]], 1)).reshape(P, KD, 2, HEADS0)
    cq, ck, cv = (a["L0_attn_conv_" + c].T for c in "qkv")
    cw = np.stack([halves(cq, 0), halves(ck, 0), halves(cv, 0), halves(cv, 1)])
    cw = cw.transpose(3, 0, 2, 1)
    invf = np.tile((1.0 / 10000.0 ** (np.arange(0, 64, 2, dtype=np.float32) / np.float32(64))).astype(np.float32), 3)
    rw = np.tile(a["L0_attn_rms_w"].reshape(PAIRS, 2), (3, 1))
    wo0 = a["L0_attn_Wo"].reshape(2, HALF, 2, D).transpose(1, 0, 2, 3)
    cent = kt(a["L0_ffn_centroids"].T)
    gb = np.tile(a["L0_ffn_gate_bias"], (P, NT, 1))
    gate = np.concatenate([a["L0_ffn_wg"], a["L0_ffn_wg_s"].reshape(D, NSHARED, P).transpose(1, 0, 2)])
    up = np.concatenate([a["L0_ffn_wu"], a["L0_ffn_wu_s"].reshape(D, NSHARED, P).transpose(1, 0, 2)])
    down = np.concatenate([a["L0_ffn_wd"], a["L0_ffn_wd_s"].reshape(NSHARED, P, D)])

    def ekt(w):
        return w.reshape(NE, KD, P, P).transpose(0, 2, 1, 3).reshape(NE, P, D)

    wexp = np.concatenate([ekt(gate), ekt(up), down], 2)
    iota = np.tile(np.arange(NEXP, dtype=np.float32), (P, NT, 1))
    lutk = np.tile(np.arange(NE, dtype=np.float32), (P, 1))
    wq1, wk1, wv1 = (a["L1_attn_W_" + c] for c in "QKV")
    qk = np.stack([wq1, wk1], 1).reshape(NPAIR, 2, 2, DH, KD, P).transpose(0, 5, 1, 2, 4, 3).reshape(NPAIR, P, -1)
    vw = wv1.reshape(NPAIR, 2, DH, KD, P).transpose(0, 4, 3, 1, 2).reshape(NPAIR, P, -1)
    ow = a["L1_attn_W_O"].reshape(D, NPAIR, 2, DH).transpose(1, 3, 2, 0).reshape(NPAIR, P, -1)
    wpair = np.concatenate([qk, vw, ow], 2)
    gi, ui, di = (a[f"L1_ffn_{n}_idx"] for n in ("gate", "up", "down"))

    def padded(idx):
        return np.concatenate([idx, np.full((INTER_PAD - INTER, D), LUTN, idx.dtype)])

    fidx = np.concatenate([kt(padded(gi).T).reshape(P, -1), kt(padded(ui).T).reshape(P, -1),
                           padded(di.T).reshape(NM, P, D).transpose(1, 0, 2).reshape(P, -1)], 1)
    fidx = fidx.reshape(P, NB, LC).transpose(1, 0, 2)
    lut = np.zeros((P, NE), np.float32)
    lut[:, :LUTN] = a["L1_ffn_lut"]

    x = a["L0_attn_hidden_states"]
    named = dict(x=np.concatenate([x, x[:1]]), w0=w0, wab=wab, cw=cw, invf=invf[:, None], rmsw=rw, wo0=wo0, cent=cent,
                 gbias=gb, wexp=wexp, iota=iota, lutk=lutk, wpair=wpair, fidx=fidx, lut=lut)
    nc = bacc.Bacc("TRN2", target_bir_lowering=False, num_devices=1)
    arrays, args = {}, []
    for name, arr in named.items():
        arr = np.ascontiguousarray(arr)
        arrays[f"in_{name}"] = arr
        args.append(nc.dram_tensor(f"in_{name}", arr.shape, mybir.dt.from_np(arr.dtype), kind="ExternalInput").ap())
    args.append(nc.dram_tensor("out_x", _OUT, F32, kind="ExternalOutput").ap())
    two_layer_program(nc, *args)
    r = run_bass_kernel_spmd(nc, [arrays], core_ids=[0])
    return r.results[0]["out_x"]
```
